# Optimizing a Trainium2 kernel written in Bass

```python
import numpy as np
import jax
import jax.numpy as jnp

def _softmax(x, axis=-1):
    return jax.nn.softmax(x, axis=axis)

def _gelu(x):
    return jax.nn.gelu(x, approximate=True)

def _silu(x):
    return jax.nn.silu(x)

def _sigmoid(x):
    return jax.nn.sigmoid(x)

def _layernorm(x, axis=-1, eps=1e-05):
    m = jnp.mean(x, axis=axis, keepdims=True)
    v = jnp.var(x, axis=axis, keepdims=True)
    return (x - m) / jnp.sqrt(v + eps)

def _scatter_add(tgt, idx, src, axis=0):
    return tgt.at[idx].add(src)

def _segment_sum(src, seg, n):
    return jax.ops.segment_sum(src, seg, n)
kernel_name = 'mk_audio_tower_d4_tok_audfeat512_r4_9f9403'

def setup_inputs(seed: int=0):
    np.random.seed(seed)
    _w = jnp.asarray

    def _rec_inputs():
        import jax
        import jax.numpy as jnp
        _rk = jax.random.key(seed)
        x = -7.10856e-05 + 0.999911 * jax.random.normal(jax.random.fold_in(_rk, 1), (64, 256, 128), jnp.float32)
        return x
    x = _rec_inputs()

    def _L0_tok_setup():
        import jax, jax.numpy as jnp
        import numpy as np
        BLOCK = 128
        TOP_K = 16
        key = jax.random.key(seed)
        k1, k2 = jax.random.split(key)
        B, S, D = (8, 4096, 128)
        x = jax.random.normal(k1, (B, S, D), dtype=jnp.float32)
        W = jax.random.normal(k2, (1, D), dtype=jnp.float32) * (1.0 / np.sqrt(D))
        b = jnp.zeros((1,), dtype=jnp.float32)
        return {'x': x, 'W': W, 'b': b}
    _L0_tok_all = _L0_tok_setup()
    _L0_tok_in = {k: v for k, v in _L0_tok_all.items() if k in ('W', 'b')}
    del _L0_tok_all

    def _L0_attn_setup():
        import jax, jax.numpy as jnp
        import numpy as np
        B, L, D_MODEL = (4, 256, 128)
        D_STATE, EXPAND, D_CONV = (16, 2, 4)
        D_INNER = EXPAND * D_MODEL
        DT_RANK = D_MODEL // 16
        NUM_LAYERS = 2
        NL2 = 2 * NUM_LAYERS

        def layer_norm(x, w, b, eps=1e-06):
            m = jnp.mean(x, -1, keepdims=True)
            v = jnp.var(x, -1, keepdims=True)
            return (x - m) * jax.lax.rsqrt(v + eps) * w + b

        def causal_conv1d(x, w, b):
            y = jax.lax.conv_general_dilated(x.transpose(0, 2, 1), w[:, None, :], (1,), [(D_CONV - 1, 0)], feature_group_count=D_INNER, dimension_numbers=('NCH', 'OIH', 'NCH'))
            return y.transpose(0, 2, 1) + b

        def selective_scan(u, dt, A, Bm, Cm, Dskip):
            dA = jnp.exp(dt[..., None] * A)
            dBu = (dt * u)[..., None] * Bm[:, :, None, :]

            def step(h, inp):
                dA_t, dBu_t, C_t = inp
                h = dA_t * h + dBu_t
                return (h, jnp.einsum('bdn,bn->bd', h, C_t))
            h0 = jnp.zeros((u.shape[0], u.shape[2], D_STATE), u.dtype)
            xs = (jnp.moveaxis(dA, 1, 0), jnp.moveaxis(dBu, 1, 0), jnp.moveaxis(Cm, 1, 0))
            _, ys = jax.lax.scan(step, h0, xs)
            return jnp.moveaxis(ys, 0, 1) + u * Dskip

        def _one_dir(x, cw, cb, xpw, dpw, dpb, A_log, Dskip):
            xc = jax.nn.silu(causal_conv1d(x, cw, cb))
            proj = xc @ xpw.T
            dt_r, Bm, Cm = jnp.split(proj, [DT_RANK, DT_RANK + D_STATE], axis=-1)
            dt = jax.nn.softplus(dt_r @ dpw.T + dpb)
            A = -jnp.exp(A_log)
            return selective_scan(xc, dt, A, Bm, Cm, Dskip)

        def _bimamba(u, i, p):
            xz = u @ p['in_proj_w'][i].T
            x, z = jnp.split(xz, 2, axis=-1)
            yf = _one_dir(x, p['conv_w'][i, 0], p['conv_b'][i, 0], p['xproj_w'][i, 0], p['dtproj_w'][i, 0], p['dtproj_b'][i, 0], p['A_log'][i, 0], p['Dskip'][i, 0])
            yb = _one_dir(x[:, ::-1], p['conv_w'][i, 1], p['conv_b'][i, 1], p['xproj_w'][i, 1], p['dtproj_w'][i, 1], p['dtproj_b'][i, 1], p['A_log'][i, 1], p['Dskip'][i, 1])[:, ::-1]
            y = (yf + yb) * jax.nn.silu(z)
            return y @ p['out_proj_w'][i].T

        def _enc_layer(a, t, i, p):
            ao = _bimamba(a, i, p)
            to = _bimamba(t, i, p)
            a_out = a + layer_norm(ao, p['ln_w'][i, 0], p['ln_b'][i, 0])
            t_out = t + layer_norm(to, p['ln_w'][i, 1], p['ln_b'][i, 1])
            return (a_out, t_out)

        def _reference_tuple_inner(a_x, v_x, t_x, in_proj_w, conv_w, conv_b, xproj_w, dtproj_w, dtproj_b, A_log, Dskip, out_proj_w, ln_w, ln_b):
            p = dict(in_proj_w=in_proj_w, conv_w=conv_w, conv_b=conv_b, xproj_w=xproj_w, dtproj_w=dtproj_w, dtproj_b=dtproj_b, A_log=A_log, Dskip=Dskip, out_proj_w=out_proj_w, ln_w=ln_w, ln_b=ln_b)
            a_out, v_out, t_out = (a_x, v_x, t_x)
            for i in range(NUM_LAYERS):
                a_out, t_at = _enc_layer(a_out, t_out, 2 * i, p)
                v_out, t_vt = _enc_layer(v_out, t_out, 2 * i + 1, p)
                t_out = (t_at + t_vt) / 2
            return (a_out, v_out, t_out)
        key = jax.random.key(seed)
        ks = jax.random.split(key, 16)
        s = 0.02
        inp = {'a_x': jax.random.normal(ks[0], (B, L, D_MODEL), jnp.float32), 'v_x': jax.random.normal(ks[1], (B, L, D_MODEL), jnp.float32), 't_x': jax.random.normal(ks[2], (B, L, D_MODEL), jnp.float32), 'in_proj_w': s * jax.random.normal(ks[3], (NL2, 2 * D_INNER, D_MODEL), jnp.float32), 'conv_w': s * jax.random.normal(ks[4], (NL2, 2, D_INNER, D_CONV), jnp.float32), 'conv_b': jnp.zeros((NL2, 2, D_INNER), jnp.float32), 'xproj_w': s * jax.random.normal(ks[5], (NL2, 2, DT_RANK + 2 * D_STATE, D_INNER), jnp.float32), 'dtproj_w': s * jax.random.normal(ks[6], (NL2, 2, D_INNER, DT_RANK), jnp.float32), 'dtproj_b': 0.1 * jax.random.normal(ks[7], (NL2, 2, D_INNER), jnp.float32), 'A_log': jnp.log(jnp.broadcast_to(jnp.arange(1.0, D_STATE + 1.0, dtype=jnp.float32), (NL2, 2, D_INNER, D_STATE))), 'Dskip': jnp.ones((NL2, 2, D_INNER), jnp.float32), 'out_proj_w': s * jax.random.normal(ks[8], (NL2, D_MODEL, D_INNER), jnp.float32), 'ln_w': jnp.ones((NL2, 2, D_MODEL), jnp.float32), 'ln_b': jnp.zeros((NL2, 2, D_MODEL), jnp.float32)}
        return inp
    _L0_attn_all = _L0_attn_setup()
    _L0_attn_in = {k: v for k, v in _L0_attn_all.items() if k in ('v_x', 't_x', 'in_proj_w', 'conv_w', 'conv_b', 'xproj_w', 'dtproj_w', 'dtproj_b', 'A_log', 'Dskip', 'out_proj_w', 'ln_w', 'ln_b')}
    del _L0_attn_all

    def _L0_ffn_setup():
        import jax, jax.numpy as jnp
        import numpy as np
        DIM = 128
        MOE_DIM = 64
        E = 64
        G = 8
        TOPK_G = 4
        K = 8
        SCALE = 2.5
        CAP = 256

        def _gate(x2, gate_w, gate_b):
            T = x2.shape[0]
            scores = jax.nn.sigmoid(x2 @ gate_w.T)
            s = (scores + gate_b).reshape(T, G, E // G)
            group_scores = jax.lax.top_k(s, 2)[0].sum(-1)
            top_groups = jax.lax.top_k(group_scores, TOPK_G)[1]
            gmask = jnp.zeros((T, G), bool).at[jnp.arange(T)[:, None], top_groups].set(True)
            s = jnp.where(gmask[..., None], s, -jnp.inf).reshape(T, E)
            idx = jax.lax.top_k(s, K)[1]
            w = jnp.take_along_axis(scores, idx, axis=1)
            w = w / w.sum(-1, keepdims=True) * SCALE
            return (w, idx)

        def _moe_forward(x, gate_w, gate_b, w1, w3, w2):
            shape = x.shape
            x2 = x.reshape(-1, DIM)
            T = x2.shape[0]
            w, idx = _gate(x2, gate_w, gate_b)
            flat_e = idx.reshape(-1)
            oh = (flat_e[:, None] == jnp.arange(E)[None, :]).astype(jnp.int32)
            pos = (jnp.cumsum(oh, axis=0) * oh).sum(-1) - 1
            x_rep = jnp.repeat(x2, K, axis=0)
            xb = jnp.zeros((E, CAP, DIM), x2.dtype).at[flat_e, pos].set(x_rep, mode='drop')
            h = jax.nn.silu(jnp.einsum('ecd,edm->ecm', xb, w1)) * jnp.einsum('ecd,edm->ecm', xb, w3)
            yb = jnp.einsum('ecm,emd->ecd', h, w2)
            y = yb.at[flat_e, pos].get(mode='fill', fill_value=0.0) * w.reshape(-1)[:, None]
            return y.reshape(T, K, DIM).sum(1).reshape(shape)
        key = jax.random.key(seed)
        ks = jax.random.split(key, 6)
        x = jax.random.normal(ks[0], (4, 128, DIM), jnp.float32)
        gate_w = jax.random.normal(ks[1], (E, DIM), jnp.float32) / np.sqrt(DIM).astype(np.float32)
        gate_b = jax.random.normal(ks[2], (E,), jnp.float32) * 0.01
        w1 = jax.random.normal(ks[3], (E, DIM, MOE_DIM), jnp.float32) / np.sqrt(DIM).astype(np.float32)
        w3 = jax.random.normal(ks[4], (E, DIM, MOE_DIM), jnp.float32) / np.sqrt(DIM).astype(np.float32)
        w2 = jax.random.normal(ks[5], (E, MOE_DIM, DIM), jnp.float32) / np.sqrt(MOE_DIM).astype(np.float32)
        return {'x': x, 'gate_w': gate_w, 'gate_b': gate_b, 'w1': w1, 'w3': w3, 'w2': w2}
    _L0_ffn_all = _L0_ffn_setup()
    _L0_ffn_in = {k: v for k, v in _L0_ffn_all.items() if k in ('gate_w', 'gate_b', 'w1', 'w3', 'w2')}
    del _L0_ffn_all

    def _L1_attn_setup():
        import jax, jax.numpy as jnp
        import numpy as np
        D_MODEL = 128
        D_IN = D_MODEL * 2
        D_STATE = 128
        D_CONV = 4
        EXPAND = 2
        D_INNER = EXPAND * D_IN
        HEADDIM = 64
        NHEADS = D_INNER // HEADDIM
        CONV_DIM = D_INNER + 2 * D_STATE
        D_PROJ = 2 * D_INNER + 2 * D_STATE + NHEADS
        BATCH, SEQ = (2, 1024)

        def layernorm(x, g, b, eps=1e-05):
            mu = x.mean(-1, keepdims=True)
            v = ((x - mu) ** 2).mean(-1, keepdims=True)
            return (x - mu) * jax.lax.rsqrt(v + eps) * g + b

        def dwconv_causal(x, w, b):
            xp = jnp.pad(x, ((0, 0), (D_CONV - 1, 0), (0, 0)))
            y = jax.lax.conv_general_dilated(xp.transpose(0, 2, 1), w[:, None, :], (1,), 'VALID', feature_group_count=w.shape[0])
            return y.transpose(0, 2, 1) + b

        def mamba2(x, win, convw, convb, dtb, Alog, Dp, normw, wout):
            zxbcdt = x @ win
            z, xBC, dt = jnp.split(zxbcdt, [D_INNER, D_INNER + CONV_DIM], axis=-1)
            dt = jax.nn.softplus(dt + dtb)
            xBC = jax.nn.silu(dwconv_causal(xBC, convw, convb))
            xs, Bm, Cm = jnp.split(xBC, [D_INNER, D_INNER + D_STATE], axis=-1)
            xs = xs.reshape(xs.shape[0], xs.shape[1], NHEADS, HEADDIM)
            A = -jnp.exp(Alog)
            decay = jnp.exp(dt * A)

            def step(h, inp):
                x_t, B_t, C_t, dt_t, dec_t = inp
                h = h * dec_t[:, :, None, None] + (dt_t[:, :, None] * x_t)[..., None] * B_t[:, None, None, :]
                y_t = jnp.einsum('bhpn,bn->bhp', h, C_t)
                return (h, y_t)
            h0 = jnp.zeros((x.shape[0], NHEADS, HEADDIM, D_STATE), x.dtype)
            seq = (xs.transpose(1, 0, 2, 3), Bm.transpose(1, 0, 2), Cm.transpose(1, 0, 2), dt.transpose(1, 0, 2), decay.transpose(1, 0, 2))
            _, ys = jax.lax.scan(step, h0, seq)
            y = ys.transpose(1, 0, 2, 3) + Dp[None, None, :, None] * xs
            y = y.reshape(y.shape[0], y.shape[1], D_INNER)
            yg = y * jax.nn.silu(z)
            yn = yg * jax.lax.rsqrt(jnp.mean(yg * yg, -1, keepdims=True) + 1e-05) * normw
            return yn @ wout

        def nbimamba2(x, pre_w, pre_b, pre_ln_g, pre_ln_b, post_w, post_b, post_ln_g, post_ln_b, win_f, convw_f, convb_f, dtb_f, Alog_f, D_f, normw_f, wout_f, win_b, convw_b, convb_b, dtb_b, Alog_b, D_b, normw_b, wout_b):
            shortcut = x
            h = layernorm(x @ pre_w + pre_b, pre_ln_g, pre_ln_b)
            gate = jax.nn.silu(h)
            out_f = mamba2(h, win_f, convw_f, convb_f, dtb_f, Alog_f, D_f, normw_f, wout_f)
            out_b = jnp.flip(mamba2(jnp.flip(h, 1), win_b, convw_b, convb_b, dtb_b, Alog_b, D_b, normw_b, wout_b), 1)
            out = layernorm((out_f * gate + out_b * gate) @ post_w + post_b, post_ln_g, post_ln_b)
            return out + shortcut
        key = jax.random.key(seed)
        ks = jax.random.split(key, 32)
        r = lambda i, shape, s=1.0: jax.random.normal(ks[i], shape, jnp.float32) * s
        inp = {'x': r(0, (BATCH, SEQ, D_MODEL))}
        inp.update(pre_w=r(1, (D_MODEL, D_IN), 0.02), pre_b=jnp.zeros(D_IN, jnp.float32), pre_ln_g=jnp.ones(D_IN, jnp.float32), pre_ln_b=jnp.zeros(D_IN, jnp.float32), post_w=r(2, (D_IN, D_MODEL), 0.02), post_b=jnp.zeros(D_MODEL, jnp.float32), post_ln_g=jnp.ones(D_MODEL, jnp.float32), post_ln_b=jnp.zeros(D_MODEL, jnp.float32))
        for j, m in enumerate(('f', 'b')):
            o = 3 + j * 8
            inp[f'win_{m}'] = r(o, (D_IN, D_PROJ), 0.02)
            inp[f'convw_{m}'] = r(o + 1, (CONV_DIM, D_CONV), 0.2)
            inp[f'convb_{m}'] = jnp.zeros(CONV_DIM, jnp.float32)
            inp[f'dtb_{m}'] = r(o + 2, (NHEADS,), 0.1)
            inp[f'Alog_{m}'] = jnp.log(jnp.arange(1, NHEADS + 1, dtype=jnp.float32))
            inp[f'D_{m}'] = jnp.ones(NHEADS, jnp.float32)
            inp[f'normw_{m}'] = jnp.ones(D_INNER, jnp.float32)
            inp[f'wout_{m}'] = r(o + 3, (D_INNER, D_IN), 0.02)
        return inp
    _L1_attn_all = _L1_attn_setup()
    _L1_attn_in = {k: v for k, v in _L1_attn_all.items() if k in ('pre_w', 'pre_b', 'pre_ln_g', 'pre_ln_b', 'post_w', 'post_b', 'post_ln_g', 'post_ln_b', 'win_f', 'convw_f', 'convb_f', 'dtb_f', 'Alog_f', 'D_f', 'normw_f', 'wout_f', 'win_b', 'convw_b', 'convb_b', 'dtb_b', 'Alog_b', 'D_b', 'normw_b', 'wout_b')}
    del _L1_attn_all

    def _L1_ffn_setup():
        import jax, jax.numpy as jnp
        import numpy as np
        B, S, D = (16, 256, 128)
        H = 512
        E = 16
        TOP_K = 4
        key = jax.random.key(seed)
        ks = jax.random.split(key, 8)
        scale = 0.02
        x = jax.random.normal(ks[0], (B, S, D), dtype=jnp.float32)
        router_w = jax.random.normal(ks[1], (D, E), dtype=jnp.float32) * scale
        router_b = jax.random.normal(ks[2], (E,), dtype=jnp.float32) * scale
        w1 = jax.random.normal(ks[3], (E, D, H), dtype=jnp.float32) * scale
        b1 = jax.random.normal(ks[4], (E, H), dtype=jnp.float32) * scale
        w2 = jax.random.normal(ks[5], (E, H, D), dtype=jnp.float32) * scale
        b2 = jax.random.normal(ks[6], (E, D), dtype=jnp.float32) * scale
        return {'x': x, 'router_w': router_w, 'router_b': router_b, 'w1': w1, 'b1': b1, 'w2': w2, 'b2': b2}
    _L1_ffn_all = _L1_ffn_setup()
    _L1_ffn_in = {k: v for k, v in _L1_ffn_all.items() if k in ('router_w', 'router_b', 'w1', 'b1', 'w2', 'b2')}
    del _L1_ffn_all

    def _L2_attn_setup():
        import jax, jax.numpy as jnp
        import numpy as np
        EPS = 1e-05
        key = jax.random.key(seed)
        ks = jax.random.split(key, 6)
        B, T, D, H = (2, 1024, 128, 8)
        bound = float(np.sqrt(6.0 / (D + D)))

        def xavier(k):
            return jax.random.uniform(k, (D, D), jnp.float32, -bound, bound)
        return {'x': jax.random.normal(ks[0], (B, T, D), jnp.float32), 'W_q': xavier(ks[1]), 'W_k': xavier(ks[2]), 'W_v': xavier(ks[3]), 'W_o': xavier(ks[4]), 'ln_gamma': jnp.ones((D,), jnp.float32), 'ln_beta': jnp.zeros((D,), jnp.float32)}
    _L2_attn_all = _L2_attn_setup()
    _L2_attn_in = {k: v for k, v in _L2_attn_all.items() if k in ('W_q', 'W_k', 'W_v', 'W_o', 'ln_gamma', 'ln_beta')}
    del _L2_attn_all

    def _L2_ffn_setup():
        import jax, jax.numpy as jnp
        import numpy as np
        B, S, D = (8, 1024, 128)
        H = 512
        O = 128
        E = 8
        TOP_K = 1
        key = jax.random.key(seed)
        ks = jax.random.split(key, 8)
        sc = 0.02
        return {'x': jax.random.normal(ks[0], (B, S, D), dtype=jnp.float32), 'Wr': jax.random.normal(ks[1], (D, E), dtype=jnp.float32) * sc, 'br': jnp.zeros((E,), dtype=jnp.float32), 'W1': jax.random.normal(ks[2], (E, D, H), dtype=jnp.float32) * sc, 'b1': jnp.zeros((E, H), dtype=jnp.float32), 'W2': jax.random.normal(ks[3], (E, H, O), dtype=jnp.float32) * sc, 'b2': jnp.zeros((E, O), dtype=jnp.float32)}
    _L2_ffn_all = _L2_ffn_setup()
    _L2_ffn_in = {k: v for k, v in _L2_ffn_all.items() if k in ('Wr', 'br', 'W1', 'b1', 'W2', 'b2')}
    del _L2_ffn_all

    def _L3_attn_setup():
        import jax, jax.numpy as jnp
        import numpy as np
        D = 128
        H = 4
        DK = D // 2
        DV = D
        HK = DK // H
        HV = DV // H
        GATE_LOW_RANK = 16
        GATE_LOGIT_NORMALIZER = 16.0
        LN_EPS = 1e-05

        def _gla(x, Wq, Wk, Wv, Wg, Wgk1, Wgk2, bgk2, Wo):
            B, S, _ = x.shape
            q = (x @ Wq).reshape(B, S, H, HK) * HK ** (-0.5)
            k = (x @ Wk).reshape(B, S, H, HK)
            v = (x @ Wv).reshape(B, S, H, HV)
            g = (x @ Wg).reshape(B, S, H, HV)
            gk = jax.nn.log_sigmoid(x @ Wgk1 @ Wgk2 + bgk2) / GATE_LOGIT_NORMALIZER
            gk = gk.reshape(B, S, H, HK)

            def step(h, inp):
                q_t, k_t, v_t, gk_t = inp
                h = jnp.exp(gk_t)[..., None] * h + k_t[..., None] * v_t[..., None, :]
                o_t = jnp.einsum('bhk,bhkv->bhv', q_t, h)
                return (h, o_t)
            h0 = jnp.zeros((B, H, HK, HV), x.dtype)
            xs = (q.swapaxes(0, 1), k.swapaxes(0, 1), v.swapaxes(0, 1), gk.swapaxes(0, 1))
            _, o = jax.lax.scan(step, h0, xs)
            o = o.swapaxes(0, 1)
            mu = o.mean(-1, keepdims=True)
            var = ((o - mu) ** 2).mean(-1, keepdims=True)
            o = (o - mu) * jax.lax.rsqrt(var + LN_EPS)
            o = o * jax.nn.silu(g)
            return o.reshape(B, S, DV) @ Wo
        key = jax.random.key(seed)
        ks = jax.random.split(key, 9)
        B, S = (2, 4096)
        g = lambda k, shape, scale: jax.random.normal(k, shape, dtype=jnp.float32) * scale
        return {'x': g(ks[0], (B, S, D), 1.0), 'Wq': g(ks[1], (D, DK), D ** (-0.5)), 'Wk': g(ks[2], (D, DK), D ** (-0.5)), 'Wv': g(ks[3], (D, DV), D ** (-0.5)), 'Wg': g(ks[4], (D, DV), D ** (-0.5)), 'Wgk1': g(ks[5], (D, GATE_LOW_RANK), D ** (-0.5)), 'Wgk2': g(ks[6], (GATE_LOW_RANK, DK), GATE_LOW_RANK ** (-0.5)), 'bgk2': jnp.zeros((DK,), jnp.float32), 'Wo': g(ks[7], (DV, D), DV ** (-0.5))}
    _L3_attn_all = _L3_attn_setup()
    _L3_attn_in = {k: v for k, v in _L3_attn_all.items() if k in ('Wq', 'Wk', 'Wv', 'Wg', 'Wgk1', 'Wgk2', 'bgk2', 'Wo')}
    del _L3_attn_all

    def _L3_ffn_setup():
        import jax, jax.numpy as jnp
        import numpy as np
        TOP_K = 2

        def quick_gelu(x):
            return x * jax.nn.sigmoid(1.702 * x)
        key = jax.random.key(seed)
        ks = jax.random.split(key, 6)
        B, S, H, I, E = (8, 1024, 128, 256, 8)
        s_h = 1.0 / np.sqrt(H).astype(np.float32)
        s_i = 1.0 / np.sqrt(I).astype(np.float32)
        return {'hidden_states': jax.random.normal(ks[0], (B, S, H), jnp.float32), 'router_w': jax.random.normal(ks[1], (H, E), jnp.float32) * s_h, 'router_b': jnp.zeros((E,), jnp.float32), 'gate_up_proj': jax.random.normal(ks[2], (E, H, 2 * I), jnp.float32) * s_h, 'gate_up_proj_bias': jnp.zeros((E, 2 * I), jnp.float32), 'down_proj': jax.random.normal(ks[3], (E, I, H), jnp.float32) * s_i, 'down_proj_bias': jnp.zeros((E, H), jnp.float32)}
    _L3_ffn_all = _L3_ffn_setup()
    _L3_ffn_in = {k: v for k, v in _L3_ffn_all.items() if k in ('router_w', 'router_b', 'gate_up_proj', 'gate_up_proj_bias', 'down_proj', 'down_proj_bias')}
    del _L3_ffn_all
    return {'x': x, 'L0_tok_W': _L0_tok_in['W'], 'L0_tok_b': _L0_tok_in['b'], 'L0_attn_v_x': _L0_attn_in['v_x'], 'L0_attn_t_x': _L0_attn_in['t_x'], 'L0_attn_in_proj_w': _L0_attn_in['in_proj_w'], 'L0_attn_conv_w': _L0_attn_in['conv_w'], 'L0_attn_conv_b': _L0_attn_in['conv_b'], 'L0_attn_xproj_w': _L0_attn_in['xproj_w'], 'L0_attn_dtproj_w': _L0_attn_in['dtproj_w'], 'L0_attn_dtproj_b': _L0_attn_in['dtproj_b'], 'L0_attn_A_log': _L0_attn_in['A_log'], 'L0_attn_Dskip': _L0_attn_in['Dskip'], 'L0_attn_out_proj_w': _L0_attn_in['out_proj_w'], 'L0_attn_ln_w': _L0_attn_in['ln_w'], 'L0_attn_ln_b': _L0_attn_in['ln_b'], 'L0_ffn_gate_w': _L0_ffn_in['gate_w'], 'L0_ffn_gate_b': _L0_ffn_in['gate_b'], 'L0_ffn_w1': _L0_ffn_in['w1'], 'L0_ffn_w3': _L0_ffn_in['w3'], 'L0_ffn_w2': _L0_ffn_in['w2'], 'L1_attn_pre_w': _L1_attn_in['pre_w'], 'L1_attn_pre_b': _L1_attn_in['pre_b'], 'L1_attn_pre_ln_g': _L1_attn_in['pre_ln_g'], 'L1_attn_pre_ln_b': _L1_attn_in['pre_ln_b'], 'L1_attn_post_w': _L1_attn_in['post_w'], 'L1_attn_post_b': _L1_attn_in['post_b'], 'L1_attn_post_ln_g': _L1_attn_in['post_ln_g'], 'L1_attn_post_ln_b': _L1_attn_in['post_ln_b'], 'L1_attn_win_f': _L1_attn_in['win_f'], 'L1_attn_convw_f': _L1_attn_in['convw_f'], 'L1_attn_convb_f': _L1_attn_in['convb_f'], 'L1_attn_dtb_f': _L1_attn_in['dtb_f'], 'L1_attn_Alog_f': _L1_attn_in['Alog_f'], 'L1_attn_D_f': _L1_attn_in['D_f'], 'L1_attn_normw_f': _L1_attn_in['normw_f'], 'L1_attn_wout_f': _L1_attn_in['wout_f'], 'L1_attn_win_b': _L1_attn_in['win_b'], 'L1_attn_convw_b': _L1_attn_in['convw_b'], 'L1_attn_convb_b': _L1_attn_in['convb_b'], 'L1_attn_dtb_b': _L1_attn_in['dtb_b'], 'L1_attn_Alog_b': _L1_attn_in['Alog_b'], 'L1_attn_D_b': _L1_attn_in['D_b'], 'L1_attn_normw_b': _L1_attn_in['normw_b'], 'L1_attn_wout_b': _L1_attn_in['wout_b'], 'L1_ffn_router_w': _L1_ffn_in['router_w'], 'L1_ffn_router_b': _L1_ffn_in['router_b'], 'L1_ffn_w1': _L1_ffn_in['w1'], 'L1_ffn_b1': _L1_ffn_in['b1'], 'L1_ffn_w2': _L1_ffn_in['w2'], 'L1_ffn_b2': _L1_ffn_in['b2'], 'L2_attn_W_q': _L2_attn_in['W_q'], 'L2_attn_W_k': _L2_attn_in['W_k'], 'L2_attn_W_v': _L2_attn_in['W_v'], 'L2_attn_W_o': _L2_attn_in['W_o'], 'L2_attn_ln_gamma': _L2_attn_in['ln_gamma'], 'L2_attn_ln_beta': _L2_attn_in['ln_beta'], 'L2_ffn_Wr': _L2_ffn_in['Wr'], 'L2_ffn_br': _L2_ffn_in['br'], 'L2_ffn_W1': _L2_ffn_in['W1'], 'L2_ffn_b1': _L2_ffn_in['b1'], 'L2_ffn_W2': _L2_ffn_in['W2'], 'L2_ffn_b2': _L2_ffn_in['b2'], 'L3_attn_Wq': _L3_attn_in['Wq'], 'L3_attn_Wk': _L3_attn_in['Wk'], 'L3_attn_Wv': _L3_attn_in['Wv'], 'L3_attn_Wg': _L3_attn_in['Wg'], 'L3_attn_Wgk1': _L3_attn_in['Wgk1'], 'L3_attn_Wgk2': _L3_attn_in['Wgk2'], 'L3_attn_bgk2': _L3_attn_in['bgk2'], 'L3_attn_Wo': _L3_attn_in['Wo'], 'L3_ffn_router_w': _L3_ffn_in['router_w'], 'L3_ffn_router_b': _L3_ffn_in['router_b'], 'L3_ffn_gate_up_proj': _L3_ffn_in['gate_up_proj'], 'L3_ffn_gate_up_proj_bias': _L3_ffn_in['gate_up_proj_bias'], 'L3_ffn_down_proj': _L3_ffn_in['down_proj'], 'L3_ffn_down_proj_bias': _L3_ffn_in['down_proj_bias']}

def reference(x, L0_tok_W, L0_tok_b, L0_attn_v_x, L0_attn_t_x, L0_attn_in_proj_w, L0_attn_conv_w, L0_attn_conv_b, L0_attn_xproj_w, L0_attn_dtproj_w, L0_attn_dtproj_b, L0_attn_A_log, L0_attn_Dskip, L0_attn_out_proj_w, L0_attn_ln_w, L0_attn_ln_b, L0_ffn_gate_w, L0_ffn_gate_b, L0_ffn_w1, L0_ffn_w3, L0_ffn_w2, L1_attn_pre_w, L1_attn_pre_b, L1_attn_pre_ln_g, L1_attn_pre_ln_b, L1_attn_post_w, L1_attn_post_b, L1_attn_post_ln_g, L1_attn_post_ln_b, L1_attn_win_f, L1_attn_convw_f, L1_attn_convb_f, L1_attn_dtb_f, L1_attn_Alog_f, L1_attn_D_f, L1_attn_normw_f, L1_attn_wout_f, L1_attn_win_b, L1_attn_convw_b, L1_attn_convb_b, L1_attn_dtb_b, L1_attn_Alog_b, L1_attn_D_b, L1_attn_normw_b, L1_attn_wout_b, L1_ffn_router_w, L1_ffn_router_b, L1_ffn_w1, L1_ffn_b1, L1_ffn_w2, L1_ffn_b2, L2_attn_W_q, L2_attn_W_k, L2_attn_W_v, L2_attn_W_o, L2_attn_ln_gamma, L2_attn_ln_beta, L2_ffn_Wr, L2_ffn_br, L2_ffn_W1, L2_ffn_b1, L2_ffn_W2, L2_ffn_b2, L3_attn_Wq, L3_attn_Wk, L3_attn_Wv, L3_attn_Wg, L3_attn_Wgk1, L3_attn_Wgk2, L3_attn_bgk2, L3_attn_Wo, L3_ffn_router_w, L3_ffn_router_b, L3_ffn_gate_up_proj, L3_ffn_gate_up_proj_bias, L3_ffn_down_proj, L3_ffn_down_proj_bias):
    import jax
    import jax.numpy as jnp

    def _L0_tok_ref(x, W, b):
        import jax, jax.numpy as jnp
        import numpy as np
        BLOCK = 128
        TOP_K = 16
        B, S, D = x.shape
        n_blocks = S // BLOCK
        scores = jnp.einsum('bsd,d->bs', x, W[0]) + b[0]
        block_scores = scores.reshape(B, n_blocks, BLOCK)
        _, top_idx = jax.lax.top_k(block_scores, TOP_K)
        offsets = (jnp.arange(n_blocks, dtype=top_idx.dtype) * BLOCK)[None, :, None]
        sel_idx = (top_idx + offsets).reshape(B, n_blocks * TOP_K)
        selected_tokens = jnp.take_along_axis(x, sel_idx[:, :, None], axis=1)
        return selected_tokens

    def _L0_attn_ref(a_x, v_x, t_x, in_proj_w, conv_w, conv_b, xproj_w, dtproj_w, dtproj_b, A_log, Dskip, out_proj_w, ln_w, ln_b):
        import jax, jax.numpy as jnp
        import numpy as np
        B, L, D_MODEL = (4, 256, 128)
        D_STATE, EXPAND, D_CONV = (16, 2, 4)
        D_INNER = EXPAND * D_MODEL
        DT_RANK = D_MODEL // 16
        NUM_LAYERS = 2
        NL2 = 2 * NUM_LAYERS

        def layer_norm(x, w, b, eps=1e-06):
            m = jnp.mean(x, -1, keepdims=True)
            v = jnp.var(x, -1, keepdims=True)
            return (x - m) * jax.lax.rsqrt(v + eps) * w + b

        def causal_conv1d(x, w, b):
            y = jax.lax.conv_general_dilated(x.transpose(0, 2, 1), w[:, None, :], (1,), [(D_CONV - 1, 0)], feature_group_count=D_INNER, dimension_numbers=('NCH', 'OIH', 'NCH'))
            return y.transpose(0, 2, 1) + b

        def selective_scan(u, dt, A, Bm, Cm, Dskip):
            dA = jnp.exp(dt[..., None] * A)
            dBu = (dt * u)[..., None] * Bm[:, :, None, :]

            def step(h, inp):
                dA_t, dBu_t, C_t = inp
                h = dA_t * h + dBu_t
                return (h, jnp.einsum('bdn,bn->bd', h, C_t))
            h0 = jnp.zeros((u.shape[0], u.shape[2], D_STATE), u.dtype)
            xs = (jnp.moveaxis(dA, 1, 0), jnp.moveaxis(dBu, 1, 0), jnp.moveaxis(Cm, 1, 0))
            _, ys = jax.lax.scan(step, h0, xs)
            return jnp.moveaxis(ys, 0, 1) + u * Dskip

        def _one_dir(x, cw, cb, xpw, dpw, dpb, A_log, Dskip):
            xc = jax.nn.silu(causal_conv1d(x, cw, cb))
            proj = xc @ xpw.T
            dt_r, Bm, Cm = jnp.split(proj, [DT_RANK, DT_RANK + D_STATE], axis=-1)
            dt = jax.nn.softplus(dt_r @ dpw.T + dpb)
            A = -jnp.exp(A_log)
            return selective_scan(xc, dt, A, Bm, Cm, Dskip)

        def _bimamba(u, i, p):
            xz = u @ p['in_proj_w'][i].T
            x, z = jnp.split(xz, 2, axis=-1)
            yf = _one_dir(x, p['conv_w'][i, 0], p['conv_b'][i, 0], p['xproj_w'][i, 0], p['dtproj_w'][i, 0], p['dtproj_b'][i, 0], p['A_log'][i, 0], p['Dskip'][i, 0])
            yb = _one_dir(x[:, ::-1], p['conv_w'][i, 1], p['conv_b'][i, 1], p['xproj_w'][i, 1], p['dtproj_w'][i, 1], p['dtproj_b'][i, 1], p['A_log'][i, 1], p['Dskip'][i, 1])[:, ::-1]
            y = (yf + yb) * jax.nn.silu(z)
            return y @ p['out_proj_w'][i].T

        def _enc_layer(a, t, i, p):
            ao = _bimamba(a, i, p)
            to = _bimamba(t, i, p)
            a_out = a + layer_norm(ao, p['ln_w'][i, 0], p['ln_b'][i, 0])
            t_out = t + layer_norm(to, p['ln_w'][i, 1], p['ln_b'][i, 1])
            return (a_out, t_out)

        def _reference_tuple_inner(a_x, v_x, t_x, in_proj_w, conv_w, conv_b, xproj_w, dtproj_w, dtproj_b, A_log, Dskip, out_proj_w, ln_w, ln_b):
            p = dict(in_proj_w=in_proj_w, conv_w=conv_w, conv_b=conv_b, xproj_w=xproj_w, dtproj_w=dtproj_w, dtproj_b=dtproj_b, A_log=A_log, Dskip=Dskip, out_proj_w=out_proj_w, ln_w=ln_w, ln_b=ln_b)
            a_out, v_out, t_out = (a_x, v_x, t_x)
            for i in range(NUM_LAYERS):
                a_out, t_at = _enc_layer(a_out, t_out, 2 * i, p)
                v_out, t_vt = _enc_layer(v_out, t_out, 2 * i + 1, p)
                t_out = (t_at + t_vt) / 2
            return (a_out, v_out, t_out)
        return _reference_tuple_inner(a_x, v_x, t_x, in_proj_w, conv_w, conv_b, xproj_w, dtproj_w, dtproj_b, A_log, Dskip, out_proj_w, ln_w, ln_b)[0]

    def _L0_ffn_ref(x, gate_w, gate_b, w1, w3, w2):
        import jax, jax.numpy as jnp
        import numpy as np
        DIM = 128
        MOE_DIM = 64
        E = 64
        G = 8
        TOPK_G = 4
        K = 8
        SCALE = 2.5
        CAP = 256

        def _gate(x2, gate_w, gate_b):
            T = x2.shape[0]
            scores = jax.nn.sigmoid(x2 @ gate_w.T)
            s = (scores + gate_b).reshape(T, G, E // G)
            group_scores = jax.lax.top_k(s, 2)[0].sum(-1)
            top_groups = jax.lax.top_k(group_scores, TOPK_G)[1]
            gmask = jnp.zeros((T, G), bool).at[jnp.arange(T)[:, None], top_groups].set(True)
            s = jnp.where(gmask[..., None], s, -jnp.inf).reshape(T, E)
            idx = jax.lax.top_k(s, K)[1]
            w = jnp.take_along_axis(scores, idx, axis=1)
            w = w / w.sum(-1, keepdims=True) * SCALE
            return (w, idx)

        def _moe_forward(x, gate_w, gate_b, w1, w3, w2):
            shape = x.shape
            x2 = x.reshape(-1, DIM)
            T = x2.shape[0]
            w, idx = _gate(x2, gate_w, gate_b)
            flat_e = idx.reshape(-1)
            oh = (flat_e[:, None] == jnp.arange(E)[None, :]).astype(jnp.int32)
            pos = (jnp.cumsum(oh, axis=0) * oh).sum(-1) - 1
            x_rep = jnp.repeat(x2, K, axis=0)
            xb = jnp.zeros((E, CAP, DIM), x2.dtype).at[flat_e, pos].set(x_rep, mode='drop')
            h = jax.nn.silu(jnp.einsum('ecd,edm->ecm', xb, w1)) * jnp.einsum('ecd,edm->ecm', xb, w3)
            yb = jnp.einsum('ecm,emd->ecd', h, w2)
            y = yb.at[flat_e, pos].get(mode='fill', fill_value=0.0) * w.reshape(-1)[:, None]
            return y.reshape(T, K, DIM).sum(1).reshape(shape)
        return _moe_forward(x, gate_w, gate_b, w1, w3, w2)

    def _L1_attn_ref(x, pre_w, pre_b, pre_ln_g, pre_ln_b, post_w, post_b, post_ln_g, post_ln_b, win_f, convw_f, convb_f, dtb_f, Alog_f, D_f, normw_f, wout_f, win_b, convw_b, convb_b, dtb_b, Alog_b, D_b, normw_b, wout_b):
        import jax, jax.numpy as jnp
        import numpy as np
        D_MODEL = 128
        D_IN = D_MODEL * 2
        D_STATE = 128
        D_CONV = 4
        EXPAND = 2
        D_INNER = EXPAND * D_IN
        HEADDIM = 64
        NHEADS = D_INNER // HEADDIM
        CONV_DIM = D_INNER + 2 * D_STATE
        D_PROJ = 2 * D_INNER + 2 * D_STATE + NHEADS
        BATCH, SEQ = (2, 1024)

        def layernorm(x, g, b, eps=1e-05):
            mu = x.mean(-1, keepdims=True)
            v = ((x - mu) ** 2).mean(-1, keepdims=True)
            return (x - mu) * jax.lax.rsqrt(v + eps) * g + b

        def dwconv_causal(x, w, b):
            xp = jnp.pad(x, ((0, 0), (D_CONV - 1, 0), (0, 0)))
            y = jax.lax.conv_general_dilated(xp.transpose(0, 2, 1), w[:, None, :], (1,), 'VALID', feature_group_count=w.shape[0])
            return y.transpose(0, 2, 1) + b

        def mamba2(x, win, convw, convb, dtb, Alog, Dp, normw, wout):
            zxbcdt = x @ win
            z, xBC, dt = jnp.split(zxbcdt, [D_INNER, D_INNER + CONV_DIM], axis=-1)
            dt = jax.nn.softplus(dt + dtb)
            xBC = jax.nn.silu(dwconv_causal(xBC, convw, convb))
            xs, Bm, Cm = jnp.split(xBC, [D_INNER, D_INNER + D_STATE], axis=-1)
            xs = xs.reshape(xs.shape[0], xs.shape[1], NHEADS, HEADDIM)
            A = -jnp.exp(Alog)
            decay = jnp.exp(dt * A)

            def step(h, inp):
                x_t, B_t, C_t, dt_t, dec_t = inp
                h = h * dec_t[:, :, None, None] + (dt_t[:, :, None] * x_t)[..., None] * B_t[:, None, None, :]
                y_t = jnp.einsum('bhpn,bn->bhp', h, C_t)
                return (h, y_t)
            h0 = jnp.zeros((x.shape[0], NHEADS, HEADDIM, D_STATE), x.dtype)
            seq = (xs.transpose(1, 0, 2, 3), Bm.transpose(1, 0, 2), Cm.transpose(1, 0, 2), dt.transpose(1, 0, 2), decay.transpose(1, 0, 2))
            _, ys = jax.lax.scan(step, h0, seq)
            y = ys.transpose(1, 0, 2, 3) + Dp[None, None, :, None] * xs
            y = y.reshape(y.shape[0], y.shape[1], D_INNER)
            yg = y * jax.nn.silu(z)
            yn = yg * jax.lax.rsqrt(jnp.mean(yg * yg, -1, keepdims=True) + 1e-05) * normw
            return yn @ wout

        def nbimamba2(x, pre_w, pre_b, pre_ln_g, pre_ln_b, post_w, post_b, post_ln_g, post_ln_b, win_f, convw_f, convb_f, dtb_f, Alog_f, D_f, normw_f, wout_f, win_b, convw_b, convb_b, dtb_b, Alog_b, D_b, normw_b, wout_b):
            shortcut = x
            h = layernorm(x @ pre_w + pre_b, pre_ln_g, pre_ln_b)
            gate = jax.nn.silu(h)
            out_f = mamba2(h, win_f, convw_f, convb_f, dtb_f, Alog_f, D_f, normw_f, wout_f)
            out_b = jnp.flip(mamba2(jnp.flip(h, 1), win_b, convw_b, convb_b, dtb_b, Alog_b, D_b, normw_b, wout_b), 1)
            out = layernorm((out_f * gate + out_b * gate) @ post_w + post_b, post_ln_g, post_ln_b)
            return out + shortcut
        return nbimamba2(x, pre_w, pre_b, pre_ln_g, pre_ln_b, post_w, post_b, post_ln_g, post_ln_b, win_f, convw_f, convb_f, dtb_f, Alog_f, D_f, normw_f, wout_f, win_b, convw_b, convb_b, dtb_b, Alog_b, D_b, normw_b, wout_b)

    def _L1_ffn_ref(x, router_w, router_b, w1, b1, w2, b2):
        import jax, jax.numpy as jnp
        import numpy as np
        B, S, D = (16, 256, 128)
        H = 512
        E = 16
        TOP_K = 4
        x_flat = x.reshape(-1, D)
        logits = x_flat @ router_w + router_b
        top_vals, top_idx = jax.lax.top_k(logits, TOP_K)
        gates = jax.nn.softmax(top_vals, axis=-1)
        onehot = jax.nn.one_hot(top_idx, E, dtype=x.dtype)
        comb = jnp.einsum('tk,tke->te', gates, onehot)
        out = jnp.zeros_like(x_flat)
        for e in range(E):
            h = jax.nn.relu(x_flat @ w1[e] + b1[e])
            y = h @ w2[e] + b2[e]
            out = out + comb[:, e:e + 1] * y
        return out.reshape(x.shape)

    def _L2_attn_ref(x, W_q, W_k, W_v, W_o, ln_gamma, ln_beta):
        import jax, jax.numpy as jnp
        import numpy as np
        EPS = 1e-05
        B, T, D = x.shape
        H = 8
        hd = D // H
        scale = jnp.sqrt(jnp.asarray(hd, x.dtype))

        def proj(W):
            y = jnp.einsum('btd,ed->bte', x, W)
            return y.reshape(B, T, H, hd).transpose(0, 2, 1, 3)
        Q, K, V = (proj(W_q), proj(W_k), proj(W_v))
        scores = jnp.einsum('bhtd,bhsd->bhts', Q, K) / scale
        attn = jax.nn.softmax(scores, axis=-1)
        ctx = jnp.einsum('bhts,bhsd->bhtd', attn, V)
        ctx = ctx.transpose(0, 2, 1, 3).reshape(B, T, D)
        out = jnp.einsum('btd,ed->bte', ctx, W_o)
        y = out + x
        mu = jnp.mean(y, axis=-1, keepdims=True)
        var = jnp.var(y, axis=-1, keepdims=True)
        return (y - mu) * jax.lax.rsqrt(var + EPS) * ln_gamma + ln_beta

    def _L2_ffn_ref(x, Wr, br, W1, b1, W2, b2):
        import jax, jax.numpy as jnp
        import numpy as np
        B, S, D = (8, 1024, 128)
        H = 512
        O = 128
        E = 8
        TOP_K = 1
        b, s, d = x.shape
        xf = x.reshape(-1, d)
        router_logits = xf @ Wr + br
        topk_logits, topk_idx = jax.lax.top_k(router_logits, TOP_K)
        topk_gates = jax.nn.softmax(topk_logits, axis=1)
        out = jnp.zeros((xf.shape[0], O), dtype=x.dtype)
        for k in range(TOP_K):
            idx_k = topk_idx[:, k]
            gate_k = topk_gates[:, k:k + 1]
            for e in range(E):
                h = jax.nn.relu(xf @ W1[e] + b1[e])
                oe = h @ W2[e] + b2[e]
                mask = (idx_k == e)[:, None]
                out = out + jnp.where(mask, gate_k * oe, 0.0)
        return out.reshape(b, s, O)

    def _L3_attn_ref(x, Wq, Wk, Wv, Wg, Wgk1, Wgk2, bgk2, Wo):
        import jax, jax.numpy as jnp
        import numpy as np
        D = 128
        H = 4
        DK = D // 2
        DV = D
        HK = DK // H
        HV = DV // H
        GATE_LOW_RANK = 16
        GATE_LOGIT_NORMALIZER = 16.0
        LN_EPS = 1e-05

        def _gla(x, Wq, Wk, Wv, Wg, Wgk1, Wgk2, bgk2, Wo):
            B, S, _ = x.shape
            q = (x @ Wq).reshape(B, S, H, HK) * HK ** (-0.5)
            k = (x @ Wk).reshape(B, S, H, HK)
            v = (x @ Wv).reshape(B, S, H, HV)
            g = (x @ Wg).reshape(B, S, H, HV)
            gk = jax.nn.log_sigmoid(x @ Wgk1 @ Wgk2 + bgk2) / GATE_LOGIT_NORMALIZER
            gk = gk.reshape(B, S, H, HK)

            def step(h, inp):
                q_t, k_t, v_t, gk_t = inp
                h = jnp.exp(gk_t)[..., None] * h + k_t[..., None] * v_t[..., None, :]
                o_t = jnp.einsum('bhk,bhkv->bhv', q_t, h)
                return (h, o_t)
            h0 = jnp.zeros((B, H, HK, HV), x.dtype)
            xs = (q.swapaxes(0, 1), k.swapaxes(0, 1), v.swapaxes(0, 1), gk.swapaxes(0, 1))
            _, o = jax.lax.scan(step, h0, xs)
            o = o.swapaxes(0, 1)
            mu = o.mean(-1, keepdims=True)
            var = ((o - mu) ** 2).mean(-1, keepdims=True)
            o = (o - mu) * jax.lax.rsqrt(var + LN_EPS)
            o = o * jax.nn.silu(g)
            return o.reshape(B, S, DV) @ Wo
        return _gla(x, Wq, Wk, Wv, Wg, Wgk1, Wgk2, bgk2, Wo)

    def _L3_ffn_ref(hidden_states, router_w, router_b, gate_up_proj, gate_up_proj_bias, down_proj, down_proj_bias):
        import jax, jax.numpy as jnp
        import numpy as np
        TOP_K = 2

        def quick_gelu(x):
            return x * jax.nn.sigmoid(1.702 * x)
        B, S, H = hidden_states.shape
        E = router_b.shape[0]
        x = hidden_states.reshape(-1, H)
        T = x.shape[0]
        logits = x @ router_w + router_b
        top_w, sel = jax.lax.top_k(logits, TOP_K)
        top_w = jax.nn.softmax(top_w, axis=-1)
        tok_w = jnp.zeros((T, E), x.dtype).at[jnp.arange(T)[:, None], sel].add(top_w)

        def body(acc, params):
            Wgu, bgu, Wd, bd, w_e = params
            gu = x @ Wgu + bgu
            gate, up = jnp.split(gu, 2, axis=-1)
            act = (up + 1.0) * quick_gelu(gate)
            out = act @ Wd + bd
            return (acc + out * w_e[:, None], None)
        acc0 = jnp.zeros((T, H), x.dtype)
        acc, _ = jax.lax.scan(body, acc0, (gate_up_proj, gate_up_proj_bias, down_proj, down_proj_bias, tok_w.T))
        return acc.reshape(B, S, H)
    h = _L0_tok_ref(x, L0_tok_W, L0_tok_b)
    h = h + _L0_attn_ref(_layernorm(h, axis=-1), L0_attn_v_x, L0_attn_t_x, L0_attn_in_proj_w, L0_attn_conv_w, L0_attn_conv_b, L0_attn_xproj_w, L0_attn_dtproj_w, L0_attn_dtproj_b, L0_attn_A_log, L0_attn_Dskip, L0_attn_out_proj_w, L0_attn_ln_w, L0_attn_ln_b)
    h = h + _L0_ffn_ref(_layernorm(h, axis=-1), L0_ffn_gate_w, L0_ffn_gate_b, L0_ffn_w1, L0_ffn_w3, L0_ffn_w2)
    h = h + _L1_attn_ref(_layernorm(h, axis=-1), L1_attn_pre_w, L1_attn_pre_b, L1_attn_pre_ln_g, L1_attn_pre_ln_b, L1_attn_post_w, L1_attn_post_b, L1_attn_post_ln_g, L1_attn_post_ln_b, L1_attn_win_f, L1_attn_convw_f, L1_attn_convb_f, L1_attn_dtb_f, L1_attn_Alog_f, L1_attn_D_f, L1_attn_normw_f, L1_attn_wout_f, L1_attn_win_b, L1_attn_convw_b, L1_attn_convb_b, L1_attn_dtb_b, L1_attn_Alog_b, L1_attn_D_b, L1_attn_normw_b, L1_attn_wout_b)
    h = h + _L1_ffn_ref(_layernorm(h, axis=-1), L1_ffn_router_w, L1_ffn_router_b, L1_ffn_w1, L1_ffn_b1, L1_ffn_w2, L1_ffn_b2)
    h = h + _L2_attn_ref(_layernorm(h, axis=-1), L2_attn_W_q, L2_attn_W_k, L2_attn_W_v, L2_attn_W_o, L2_attn_ln_gamma, L2_attn_ln_beta)
    h = h + _L2_ffn_ref(_layernorm(h, axis=-1), L2_ffn_Wr, L2_ffn_br, L2_ffn_W1, L2_ffn_b1, L2_ffn_W2, L2_ffn_b2)
    h = h + _L3_attn_ref(_layernorm(h, axis=-1), L3_attn_Wq, L3_attn_Wk, L3_attn_Wv, L3_attn_Wg, L3_attn_Wgk1, L3_attn_Wgk2, L3_attn_bgk2, L3_attn_Wo)
    h = h + _L3_ffn_ref(_layernorm(h, axis=-1), L3_ffn_router_w, L3_ffn_router_b, L3_ffn_gate_up_proj, L3_ffn_gate_up_proj_bias, L3_ffn_down_proj, L3_ffn_down_proj_bias)
    return h

_drawn_inputs = setup_inputs


def setup_inputs(seed=0):
    import zlib

    import numpy as np

    out = dict(_drawn_inputs(seed))
    spreads = {'L0_attn_conv_b': (0.0, 0.1),
     'L0_attn_Dskip': (1.0, 0.2),
     'L0_attn_ln_w': (1.0, 0.2),
     'L0_attn_ln_b': (0.0, 0.1),
     'L1_attn_pre_b': (0.0, 0.1),
     'L1_attn_pre_ln_g': (1.0, 0.2),
     'L1_attn_pre_ln_b': (0.0, 0.1),
     'L1_attn_post_b': (0.0, 0.1),
     'L1_attn_post_ln_g': (1.0, 0.2),
     'L1_attn_post_ln_b': (0.0, 0.1),
     'L1_attn_convb_f': (0.0, 0.1),
     'L1_attn_D_f': (1.0, 0.2),
     'L1_attn_normw_f': (1.0, 0.2),
     'L1_attn_convb_b': (0.0, 0.1),
     'L1_attn_D_b': (1.0, 0.2),
     'L1_attn_normw_b': (1.0, 0.2),
     'L2_attn_ln_gamma': (1.0, 0.2),
     'L2_attn_ln_beta': (0.0, 0.1),
     'L2_ffn_br': (0.0, 0.317),
     'L2_ffn_b1': (0.0, 0.745),
     'L2_ffn_b2': (0.0, 0.277),
     'L3_attn_bgk2': (0.0, 2.0),
     'L3_ffn_router_b': (0.0, 0.1),
     'L3_ffn_gate_up_proj_bias': (0.0, 0.443),
     'L3_ffn_down_proj_bias': (0.0, 0.511)}
    factors = {'L0_attn_xproj_w': 8.0,
     'L0_attn_dtproj_w': 27.323,
     'L0_attn_dtproj_b': 8.0,
     'L0_attn_A_log': 8.0,
     'L1_attn_dtb_f': 34.992,
     'L1_attn_Alog_f': 52.352,
     'L1_attn_dtb_b': 43.611,
     'L1_attn_Alog_b': 53.575,
     'L1_ffn_router_w': 3.87,
     'L1_ffn_router_b': 8.0,
     'L1_ffn_w1': 3.932,
     'L1_ffn_b1': 8.0,
     'L1_ffn_w2': 3.633,
     'L1_ffn_b2': 8.0,
     'L2_ffn_W1': 3.349,
     'L3_attn_Wgk1': 3.395,
     'L3_attn_Wgk2': 3.926}
    for name, (base, spread) in spreads.items():
        noise = np.random.default_rng([zlib.crc32(name.encode()), seed]).standard_normal(out[name].shape)
        drawn = base * np.exp(spread * noise) if base else spread * noise
        out[name] = jnp.asarray(drawn.astype(out[name].dtype))
    for name, factor in factors.items():
        out[name] = (out[name] * factor).astype(out[name].dtype)
    return out
```

```python
from contextlib import ExitStack

import numpy as np
import concourse.bass as bass
from concourse import mybir

F32 = mybir.dt.float32
BF16 = mybir.dt.bfloat16
F32R = mybir.dt.float32r
U32 = mybir.dt.uint32
ALU = mybir.AluOpType
ACT = mybir.ActivationFunctionType
AX = mybir.AxisListType

P = 128
SEQS, L = 64, 32
T = SEQS * L
TILES = T // P
QUADS = P // L
GROUP = 512
GROUPS = T // GROUP
GT = GROUP // P
HALF = T // 2


class Chain:

    def __init__(self, eng, sem):
        self.eng, self.sem, self.n = eng, sem, 0

    def __call__(self, ins):
        ins.then_inc(self.sem, 1)
        self.n += 1
        self.eng.wait_ge(self.sem, self.n)


class Stage:
    spent = []

    def __init__(self, nc, name):
        self.nc, self.name, self.ctx = nc, name, ExitStack()

    def __enter__(self):
        self.ctx.__enter__()
        return self

    def __exit__(self, *a):
        return self.ctx.__exit__(*a)

    def sb(self, name, shape, dt=F32):
        return self.ctx.enter_context(self.nc.sbuf_tensor(f"{self.name}_{name}", shape, dt))

    def ps(self, name, shape, dt=F32):
        return self.ctx.enter_context(self.nc.psum_tensor(f"{self.name}_{name}", shape, dt))

    def sem(self, name):
        s = self.nc.alloc_semaphore(f"{self.name}_{name}")
        Stage.spent.append(s)
        return s


def recycle(nc):
    nc.clear_and_free_semaphores(Stage.spent)
    Stage.spent = []
    nc.all_engine_barrier()


def spread(col, n):
    return col.unsqueeze(len(col.shape)).broadcast_to(list(col.shape) + [n])


def normalise(nc, name, H, XT, ident, XN=None, eps=1e-5):
    with Stage(nc, name) as st:
        centred = st.sb("centred", [P, TILES, P])
        xn = XN if XN is not None else st.sb("xn", [P, TILES, P])
        square = st.sb("square", [P, TILES, P])
        mean = st.sb("mean", [P, TILES])
        var = st.sb("var", [P, TILES])
        rstd = st.sb("rstd", [P, TILES])
        turned = st.ps("turned", [P, GROUPS, GROUP])
        centred_ready = st.sem("centred_ready")
        squared = st.sem("squared")
        var_ready = st.sem("var_ready")
        root_ready = st.sem("root_ready")
        xn_ready = st.sem("xn_ready")
        turned_ready = st.sem("turned_ready")
        dve_chain = st.sem("dve_chain")

        def tiles(g):
            return slice(g * GT, (g + 1) * GT)

        with nc.Block() as block:
            @block.vector
            def _(dve):
                link = Chain(dve, dve_chain)
                for g in range(GROUPS):
                    s = tiles(g)
                    link(nc.vector.tensor_reduce(mean[:, s], H[:, s, :], AX.X, ALU.add))
                    link(nc.vector.tensor_scalar(mean[:, s], mean[:, s], 1.0 / P, None, ALU.mult))
                    nc.vector.tensor_tensor(centred[:, s, :], H[:, s, :], spread(mean[:, s], P),
                                            ALU.subtract).then_inc(centred_ready, 1)
                for g in range(GROUPS):
                    s = tiles(g)
                    dve.wait_ge(squared, g + 1)
                    link(nc.vector.tensor_reduce(var[:, s], square[:, s, :], AX.X, ALU.add))
                    nc.vector.tensor_scalar(var[:, s], var[:, s], 1.0 / P, eps, ALU.mult,
                                            ALU.add).then_inc(var_ready, 1)
                for g in range(GROUPS):
                    s = tiles(g)
                    dve.wait_ge(root_ready, g + 1)
                    link(nc.vector.reciprocal(rstd[:, s], rstd[:, s]))
                    nc.vector.tensor_tensor(xn[:, s, :], centred[:, s, :], spread(rstd[:, s], P),
                                            ALU.mult).then_inc(xn_ready, 1)

            @block.scalar
            def _(act):
                for g in range(GROUPS):
                    s = tiles(g)
                    act.wait_ge(centred_ready, g + 1)
                    nc.scalar.activation(square[:, s, :], centred[:, s, :], ACT.Square).then_inc(squared, 1)
                for g in range(GROUPS):
                    s = tiles(g)
                    act.wait_ge(var_ready, g + 1)
                    nc.scalar.activation(rstd[:, s], var[:, s], ACT.Sqrt).then_inc(root_ready, 1)
                for g in range(GROUPS):
                    act.wait_ge(turned_ready, g + 1)
                    nc.scalar.activation(XT[:, g * GROUP:(g + 1) * GROUP], turned[:, g, :], ACT.Copy)

            @block.tensor
            def _(pe):
                for g in range(GROUPS):
                    pe.wait_ge(xn_ready, g + 1)
                    for t in range(GT):
                        mm = pe.transpose(turned[:, g, t * P:(t + 1) * P], xn[:, g * GT + t, :], ident[:, :])
                    mm.then_inc(turned_ready, 1)


def add_turned(nc, name, H, OT, ident):
    with Stage(nc, name) as st:
        turned = st.ps("turned", [P, GROUPS, GROUP])
        turned_ready = st.sem("turned_ready")
        with nc.Block() as block:
            @block.tensor
            def _(pe):
                for g in range(GROUPS):
                    for t in range(GT):
                        i = g * GT + t
                        mm = pe.transpose(turned[:, g, t * P:(t + 1) * P], OT[:, i * P:(i + 1) * P], ident[:, :])
                    mm.then_inc(turned_ready, 1)

            @block.vector
            def _(dve):
                for g in range(GROUPS):
                    s = slice(g * GT, (g + 1) * GT)
                    dve.wait_ge(turned_ready, g + 1)
                    nc.vector.tensor_tensor(H[:, s, :], H[:, s, :],
                                            turned[:, g, :].rearrange("p (t c) -> p t c", c=P), ALU.add)


def route_softmax(nc, name, XT, XR, ident, iota, w_router, b_router, E, K, gateT, gateF, weights, bias):
    with Stage(nc, name) as st:
        wr = st.sb("wr", [P, E])
        br = st.sb("br", [P, E])
        logits = st.sb("logits", [P, TILES, E])
        top = st.sb("top", [P, TILES, 8])
        where = st.sb("where", [P, TILES, 8], U32)
        wheref = st.sb("wheref", [P, TILES, 8])
        e = st.sb("e", [P, TILES, K])
        total = st.sb("total", [P, TILES])
        gates = st.sb("gates", [P, TILES, P])
        part16 = st.sb("part16", [P, TILES, E], BF16)
        rest = st.sb("rest", [P, TILES, E])
        picked = st.sb("picked", [P, TILES, E])
        pl = st.ps("pl", [P, TILES, E])
        turned = st.ps("turned", [P, GROUPS, GROUP])
        loaded = st.sem("loaded")
        x_rounded = st.sem("x_rounded")
        logits_ready = st.sem("logits_ready")
        shifted = st.sem("shifted")
        exps_ready = st.sem("exps_ready")
        gates_ready = st.sem("gates_ready")
        turned_ready = st.sem("turned_ready")
        chain = st.sem("chain")
        with nc.Block() as block:
            @block.sync
            def _(sp):
                sp.dma_start(wr[:, :], w_router[:, :]).then_inc(loaded, 16)
                sp.dma_start(br[:, :], b_router.partition_broadcast(P)).then_inc(loaded, 16)
                weights.start_loads(sp)

            @block.gpsimd
            def _(pool):
                split_x(nc, XT, XR, x_rounded, pool, None)
                weights.start_splits(pool, bias)

            @block.tensor
            def _(pe):
                pe.wait_ge(loaded, 32)
                for t in range(TILES):
                    mm = pe.matmul(pl[:, t, :], XT[:, t * P:(t + 1) * P], wr[:, :], start=True, stop=True)
                mm.then_inc(logits_ready, 1)
                pe.wait_ge(gates_ready, 1)
                for g in range(GROUPS):
                    for t in range(GT):
                        mm = pe.transpose(turned[:, g, t * P:(t + 1) * P], gates[:, g * GT + t, :], ident[:, :])
                    mm.then_inc(turned_ready, 1)

            @block.vector
            def _(dve):
                link = Chain(dve, chain)
                link(nc.vector.memset(gates[:, :, :], 0.0))
                dve.wait_ge(logits_ready, 1)
                dve.wait_ge(loaded, 32)
                link(nc.vector.tensor_tensor(logits[:, :, :], pl[:, :, :],
                                             br[:, :].unsqueeze(1).broadcast_to([P, TILES, E]), ALU.add))
                for t in range(TILES):
                    m = nc.vector.max(top[:, t, :], logits[:, t, :])
                link(m)
                for t in range(TILES):
                    m = nc.vector.max_index(where[:, t, :], top[:, t, :], logits[:, t, :])
                link(m)
                link(nc.vector.tensor_copy(wheref[:, :, :], where[:, :, :]))
                nc.vector.tensor_tensor(e[:, :, :], top[:, :, 0:K], spread(top[:, :, 0], K),
                                        ALU.subtract).then_inc(shifted, 1)
                dve.wait_ge(exps_ready, 1)
                link(nc.vector.tensor_reduce(total[:, :], e[:, :, :], AX.X, ALU.add))
                link(nc.vector.reciprocal(total[:, :], total[:, :]))
                link(nc.vector.tensor_tensor(e[:, :, :], e[:, :, :], spread(total[:, :], K), ALU.mult))
                for k in range(K):
                    link(nc.vector.tensor_tensor(picked[:, :, :], iota[:, 0:E].unsqueeze(1).broadcast_to([P, TILES, E]),
                                                 spread(wheref[:, :, k], E), ALU.is_equal))
                    link(nc.vector.tensor_tensor(picked[:, :, :], picked[:, :, :], spread(e[:, :, k], E), ALU.mult))
                    link(nc.vector.tensor_tensor(gates[:, :, 96:96 + E], gates[:, :, 96:96 + E], picked[:, :, :], ALU.add))
                split_gates(nc, link, gates[:, :, 96:96 + E], [gates[:, :, 32 * i:32 * i + E] for i in range(3)],
                            part16[:, :, :], rest[:, :, :]).then_inc(gates_ready, 1)

            @block.scalar
            def _(act):
                split_x(nc, XT, XR, x_rounded, None, act)
                act.wait_ge(shifted, 1)
                nc.scalar.activation(e[:, :, :], e[:, :, :], ACT.Exp).then_inc(exps_ready, 1)
                for g in range(GROUPS):
                    act.wait_ge(turned_ready, g + 1)
                    s = slice(g * GROUP, (g + 1) * GROUP)
                    nc.scalar.activation(gateT[:, s], turned[0:96, g, :], ACT.Copy)
                    nc.scalar.activation(gateF[:, s], turned[96:96 + E, g, :], ACT.Copy)


def split_gates(nc, link, value, parts, part16, rest):
    link(nc.vector.tensor_copy(part16, value))
    link(nc.vector.tensor_copy(parts[0], part16))
    link(nc.vector.tensor_tensor(rest, value, part16, ALU.subtract))
    link(nc.vector.tensor_copy(part16, rest))
    link(nc.vector.tensor_copy(parts[1], part16))
    return nc.vector.tensor_tensor(parts[2], rest, part16, ALU.subtract)


def split_parts(st):
    return st.sb("rest", [96, GROUP]), st.sb("middle", [96, GROUP], BF16)


def split(nc, link, parts, value, out):
    rest, middle = parts
    link(nc.vector.tensor_copy(out, value))
    link(nc.vector.tensor_tensor(rest[:, :], value, out, ALU.subtract))
    link(nc.vector.tensor_copy(middle[:, :], rest[:, :]))
    link(nc.vector.tensor_copy(out[32:64], middle[32:64, :]))
    link(nc.vector.tensor_tensor(out[64:96], rest[64:96, :], middle[64:96, :], ALU.subtract))


def split_x(nc, XT, XR, first_done, pool, act):
    if act is not None:
        nc.scalar.activation(XR[:, 0, :], XT[:, :], ACT.Copy).then_inc(first_done, 1)
    else:
        pool.wait_ge(first_done, 1)
        nc.gpsimd.tensor_tensor(XR[:, 1, :], XT[:, :], XR[:, 0, :].bitcast(F32), ALU.subtract)


def product(pe, out, lhsT, rhs, start=True, stop=True):
    pe.matmul(out, lhsT[0], rhs[0], start=start, stop=False, skip_group_check=True)
    pe.matmul(out, lhsT[1], rhs[0], start=False, stop=False, skip_group_check=True)
    return pe.matmul(out, lhsT[0], rhs[1], start=False, stop=stop, skip_group_check=True)


class Weights:

    def __init__(self, nc, st, source, buffers, split, biases):
        self.nc, self.source, self.buffers, self.cut, self.biases = nc, source, buffers, split, biases
        self.W = st.sb("W", [P, buffers, source.shape[-1]])
        self.WR = st.sb("WR", [P, buffers, 2, split], F32R)
        self.ZERO = st.sb("ZERO", [P, split])
        self.BX = st.sb("BX", [P, buffers, biases]) if biases else None
        self.loaded = [st.sem(f"w_loaded{j}") for j in range(buffers)]
        self.zeroed = st.sem("zeroed")
        self.rounded = st.sem("w_rounded")
        self.split_made = st.sem("w_split")
        self.bias_ready = st.sem("bias_ready")

    def load(self, sp, row, j):
        sp.dma_start(self.W[:, j, :], self.source[bass.ds(row, 1)].rearrange("u p n -> p (u n)")).then_inc(self.loaded[j], 16)

    def split(self, pool, j, n, bias):
        pool.tensor_tensor(self.WR[:, j, 0, :], self.W[:, j, 0:self.cut], self.ZERO[:, :], ALU.add).then_inc(self.rounded, 1)
        if self.biases:
            bias(self, pool, j)
        pool.wait_ge(self.rounded, n + 1)
        pool.tensor_tensor(self.WR[:, j, 1, :], self.W[:, j, 0:self.cut], self.WR[:, j, 0, :].bitcast(F32),
                           ALU.subtract).then_inc(self.split_made, 1)

    def start_loads(self, sp):
        for j in range(self.buffers):
            self.load(sp, j, j)

    def start_splits(self, pool, bias):
        pool.memset(self.ZERO[:, :], 0.0).then_inc(self.zeroed, 1)
        pool.wait_ge(self.zeroed, 1)
        pool.sem_inc(self.split_made, self.buffers)
        for j in range(self.buffers):
            pool.wait_ge(self.loaded[j], 16)
            self.split(pool, j, j, bias)


def relu_bias(weights, pool, j):
    pool.tensor_copy(weights.BX[:, j, :], weights.W[:, j, weights.cut:]).then_inc(weights.bias_ready, 1)


def quick_bias(weights, pool, j):
    gate, up = (weights.W[:, j, 3 * P + n:3 * P + n + 1] for n in range(2))
    pool.tensor_copy(weights.BX[:, j, 0:1], gate)
    pool.tensor_scalar(weights.BX[:, j, 1:2], gate, 1.702, None, ALU.mult)
    pool.tensor_scalar(weights.BX[:, j, 2:3], up, 1.0, None, ALU.add).then_inc(weights.bias_ready, 1)


def relu_experts(nc, name, XR, OT, gateT, gateF, selector, weights, b2, E):
    C = 4
    G = HALF // GROUP
    SPE = G * C
    LAG = 3
    WR, BJ = weights.WR, weights.BX
    with Stage(nc, name) as st:
        B2 = st.sb("B2", [E, P])
        R = st.sb("R", [P, 2, GROUP])
        HF = st.sb("HF", [P, 2, GROUP])
        HS = st.sb("HS", [P, 4, 2, GROUP], F32R)
        acc = st.ps("acc", [P, G, GROUP])
        ph = [st.ps(f"ph{i}", [P, GROUP]) for i in range(4)]
        pg = [st.ps(f"pg{i}", [P, GROUP]) for i in range(2)]
        bias_loaded = st.sem("bias_loaded")
        w_loaded, w_split = weights.loaded, weights.split_made
        h_ready = st.sem("h_ready")
        relu_ready = st.sem("relu_ready")
        gated = st.sem("gated")
        high_made = st.sem("high_made")
        low_made = st.sem("low_made")
        summed = st.sem("summed")
        acc_ready = st.sem("acc_ready")
        acc_read = st.sem("acc_read")
        PAIRS = E // 2
        STEPS = 2 * SPE

        def lagged(eng, half, lag, ahead, behind):
            for k in range(lag):
                ahead(0, k, half)
            with eng.Fori(0, PAIRS - 1) as i:
                for k in range(STEPS):
                    if k + lag < STEPS:
                        ahead(i, k + lag, half)
                    else:
                        ahead(i + 1, k + lag - STEPS, half)
                    behind(i, k, half)
            for k in range(STEPS):
                if k + lag < STEPS:
                    ahead(PAIRS - 1, k + lag, half)
                behind(PAIRS - 1, k, half)

        def count(i, k, half):
            return i * STEPS + (half * E * SPE + k)

        with nc.Block() as block:
            @block.sync
            def _(sp):
                sp.dma_start(B2[:, :], b2[:, :]).then_inc(bias_loaded, 16)
                for half in range(2):
                    with sp.Fori(1 - half, PAIRS) as i:
                        for j in range(2):
                            sp.wait_ge(w_split, i * 2 + (half * E + j + 1))
                            weights.load(sp, i * 2 + j, j)

            @block.gpsimd
            def _(pool):
                for half in range(2):
                    with pool.Fori(1 - half, PAIRS) as i:
                        for j in range(2):
                            pool.wait_ge(w_loaded[j], i * 16 + (half * PAIRS * 16 + 16))
                            pool.wait_ge(summed, i * STEPS + (half * E * SPE + j * SPE + 4))
                            weights.split(nc.gpsimd, j, i * 2 + (half * E + j), relu_bias)

            @block.tensor
            def _(pe):
                def first(i, k, half):
                    j, g, c = k // SPE, k % SPE // C, k % C
                    s = count(i, k, half)
                    tok = slice(half * HALF + g * GROUP, half * HALF + (g + 1) * GROUP)
                    if g == 0 and c == 0:
                        pe.wait_ge(w_split, i * 2 + (half * E + j + 3))
                    if c == 0:
                        pe.wait_ge(gated, s + 4)
                        pe.matmul(pg[(k // C) % 2][:, :], selector[:, bass.ds(i * 2 + j, 1), :].rearrange("r a c -> r (a c)"),
                                  gateT[:, tok], start=True, stop=True)
                    pe.wait_ge(relu_ready, s + 1)
                    product(pe, ph[k % 4][:, :], [WR[:, j, n, c * P:(c + 1) * P] for n in range(2)],
                            [XR[:, n, tok] for n in range(2)]).then_inc(h_ready, 1)

                def second(i, k, half):
                    j, g, c = k // SPE, k % SPE // C, k % C
                    pe.wait_ge(low_made, count(i, k, half) + 3)
                    w2 = [WR[:, j, n, (C + c) * P:(C + c + 1) * P] for n in range(2)]
                    product(pe, acc[:, g, :], w2, [HS[:, k % 4, n, :] for n in range(2)], False, False).then_inc(summed, 1)

                pe.sem_inc(summed, 4 + SPE)
                pe.wait_ge(bias_loaded, 16)
                for half in range(2):
                    if half:
                        pe.wait_ge(acc_read, 1)
                    for g in range(G):
                        tok = half * HALF + g * GROUP
                        pe.matmul(acc[:, g, :], B2[:, :], gateF[:, tok:tok + GROUP], start=True, stop=False,
                                  skip_group_check=True)
                    lagged(pe, half, LAG, first, second)
                    pe.wait_ge(summed, (half + 1) * E * SPE + 4 + SPE)
                    pe.sem_inc(acc_ready, 1)

            @block.scalar
            def _(act):
                def relu(i, k, half):
                    j, c = k // SPE, k % C
                    s = count(i, k, half)
                    act.wait_ge(h_ready, s + 1)
                    act.wait_ge(gated, s + 7)
                    nc.scalar.activation(R[:, k % 2, :], ph[k % 4][:, :], ACT.Relu,
                                         bias=BJ[:, j, c:c + 1]).then_inc(relu_ready, 1)

                def high(i, k, half):
                    s = count(i, k, half)
                    act.wait_ge(gated, s + 9)
                    act.wait_ge(summed, s + 1 + SPE)
                    nc.scalar.activation(HS[:, k % 4, 0, :], HF[:, k % 2, :], ACT.Copy).then_inc(high_made, 1)

                act.sem_inc(relu_ready, 4)
                act.sem_inc(high_made, 2)
                for half in range(2):
                    lagged(act, half, 1, relu, high)
                    act.wait_ge(acc_ready, half + 1)
                    nc.scalar.activation(OT[:, half * HALF:(half + 1) * HALF],
                                         acc[:, :, :].rearrange("p g n -> p (g n)"), ACT.Copy).then_inc(acc_read, 1)

            @block.vector
            def _(dve):
                def gate(i, k, half):
                    s = count(i, k, half)
                    dve.wait_ge(relu_ready, s + 5)
                    dve.wait_ge(high_made, s + 1)
                    dve.wait_ge(low_made, s + 1)
                    nc.vector.tensor_tensor(HF[:, k % 2, :], R[:, k % 2, :], pg[(k // C) % 2][:, :],
                                            ALU.mult).then_inc(gated, 1)

                def low(i, k, half):
                    s = count(i, k, half)
                    dve.wait_ge(high_made, s + 3)
                    nc.vector.tensor_tensor(HS[:, k % 4, 1, :], HF[:, k % 2, :], HS[:, k % 4, 0, :].bitcast(F32),
                                            ALU.subtract).then_inc(low_made, 1)

                dve.sem_inc(gated, 8)
                dve.sem_inc(low_made, 2)
                for half in range(2):
                    lagged(dve, half, 1, gate, low)


def gated_experts(nc, name, XR, OT, gateT, gateF, selector, sel_at, weights, b2, sections, quick):
    N = 16
    B = 4
    TURNS = N // B
    G = HALF // GROUP
    STEPS = B * G
    LAG = 2
    W, WR, BX = weights.W, weights.WR, weights.BX
    with Stage(nc, name) as st:
        if quick:
            B2 = st.sb("B2", [8, P])
            T1 = st.sb("T1", [P, GROUP])
        else:
            zeros = st.sb("zeros", [96, P], BF16)
        S = st.sb("S", [P, 2, GROUP])
        T2 = st.sb("T2", [P, 2, GROUP])
        HF = st.sb("HF", [P, 2, GROUP])
        HS = st.sb("HS", [P, 2, 2, GROUP], F32R)
        acc = st.ps("acc", [P, G, GROUP])
        pa = [st.ps(f"pa{i}", [P, GROUP]) for i in range(2)]
        pb = [st.ps(f"pb{i}", [P, GROUP]) for i in range(2)]
        pg = [st.ps(f"pg{i}", [P, GROUP]) for i in range(2)]
        opened = st.sem("opened")
        w_loaded, w_split, bias_ready = weights.loaded, weights.split_made, weights.bias_ready
        a_ready = st.sem("a_ready")
        b_ready = st.sem("b_ready")
        s_ready = st.sem("s_ready")
        t1_ready = st.sem("t1_ready")
        t2_ready = st.sem("t2_ready")
        gated = st.sem("gated")
        high_made = st.sem("high_made")
        low_made = st.sem("low_made")
        summed = st.sem("summed")
        acc_ready = st.sem("acc_ready")
        acc_read = st.sem("acc_read")
        WR_FREE = G * (B - 1)
        runs = [(r, half, sec) for r, (half, sec) in enumerate((h, c) for h in range(2) for c in range(sections))]

        def lagged(eng, run, lag, ahead, behind):
            for k in range(lag):
                ahead(0, k, run)
            with eng.Fori(0, TURNS - 1) as i:
                for k in range(STEPS):
                    if k + lag < STEPS:
                        ahead(i, k + lag, run)
                    else:
                        ahead(i + 1, k + lag - STEPS, run)
                    behind(i, k, run)
            for k in range(STEPS):
                if k + lag < STEPS:
                    ahead(TURNS - 1, k + lag, run)
                behind(TURNS - 1, k, run)

        def count(i, k, run):
            return i * STEPS + (run[0] * N * G + k)

        def no_split(i, k, run):
            pass

        def unit(i, j, run):
            return i * B + (run[0] * N + j)

        with nc.Block() as block:
            @block.sync
            def _(sp):
                if quick:
                    sp.dma_start(B2[:, :], b2[:, :]).then_inc(opened, 16)
                for run in runs:
                    with sp.Fori(0 if run[0] else 1, TURNS) as i:
                        for j in range(B):
                            sp.wait_ge(w_split, unit(i, j, run) + 1)
                            if quick:
                                sp.wait_ge(summed, unit(i, j, run) * G + 2)
                            weights.load(sp, i * B + (run[2] * N + j), j)

            @block.gpsimd
            def _(pool):
                for run in runs:
                    with pool.Fori(0 if run[0] else 1, TURNS) as i:
                        for j in range(B):
                            pool.wait_ge(w_loaded[j], i * 16 + (run[0] * TURNS * 16 + 16))
                            pool.wait_ge(summed, unit(i, j, run) * G + 2)
                            weights.split(nc.gpsimd, j, unit(i, j, run), quick_bias)

            @block.tensor
            def _(pe):
                def first(i, k, run):
                    r, half, sec = run
                    j, g = k // G, k % G
                    s = count(i, k, run)
                    tok = slice(half * HALF + g * GROUP, half * HALF + (g + 1) * GROUP)
                    if g == 0:
                        pe.wait_ge(w_split, unit(i, j, run) + 1 + B)
                    pe.wait_ge(gated, s + 1)
                    pe.matmul(pg[k % 2][:, :], selector[:, bass.ds(sel_at(i * B + j, i, j), 1), :].rearrange("r a c -> r (a c)"),
                              gateT[:, sec, tok], start=True, stop=True)
                    x = [XR[:, n, tok] for n in range(2)]
                    product(pe, pa[k % 2][:, :], [WR[:, j, n, 0:P] for n in range(2)], x).then_inc(a_ready, 1)
                    product(pe, pb[k % 2][:, :], [WR[:, j, n, P:2 * P] for n in range(2)], x).then_inc(b_ready, 1)

                def second(i, k, run):
                    j, g = k // G, k % G
                    if quick:
                        pe.wait_ge(gated, count(i, k, run) + 3)
                        pe.matmul(acc[:, g, :], W[:, j, 2 * P:3 * P], HF[:, k % 2, :], start=False, stop=False,
                                  skip_group_check=True).then_inc(summed, 1)
                        return
                    pe.wait_ge(low_made, count(i, k, run) + 3)
                    product(pe, acc[:, g, :], [WR[:, j, n, 2 * P:3 * P] for n in range(2)],
                            [HS[:, k % 2, n, :] for n in range(2)], False, False).then_inc(summed, 1)

                pe.sem_inc(summed, 2 + WR_FREE)
                pe.wait_ge(opened, 16 if quick else 1)
                for run in runs:
                    r, half, sec = run
                    if sec == 0:
                        if half:
                            pe.wait_ge(acc_read, 1)
                        for g in range(G):
                            tok = slice(half * HALF + g * GROUP, half * HALF + (g + 1) * GROUP)
                            if quick:
                                pe.matmul(acc[:, g, :], B2[:, :], gateF[:, tok], start=True, stop=False,
                                          skip_group_check=True)
                            else:
                                pe.matmul(acc[:, g, :], zeros[:, :], gateT[:, sec, tok], start=True, stop=False,
                                          skip_group_check=True)
                    lagged(pe, run, LAG, first, second)
                    if sec == sections - 1:
                        pe.wait_ge(summed, (r + 1) * N * G + 2 + WR_FREE)
                        pe.sem_inc(acc_ready, 1)

            @block.scalar
            def _(act):
                def bend(i, k, run):
                    j = k // G
                    s = count(i, k, run)
                    act.wait_ge(a_ready, s + 1)
                    act.wait_ge(gated, s + 1)
                    if quick:
                        if k % G == 0:
                            act.wait_ge(bias_ready, unit(i, j, run) + 1)
                        nc.scalar.activation(S[:, k % 2, :], pa[k % 2][:, :], ACT.Sigmoid, scale=1.702,
                                             bias=BX[:, j, 1:2]).then_inc(s_ready, 1)
                    else:
                        nc.scalar.activation(S[:, k % 2, :], pa[k % 2][:, :], ACT.Silu).then_inc(s_ready, 1)

                def high(i, k, run):
                    s = count(i, k, run)
                    act.wait_ge(gated, s + 3)
                    act.wait_ge(summed, s + 1 + WR_FREE)
                    nc.scalar.activation(HS[:, k % 2, 0, :], HF[:, k % 2, :], ACT.Copy).then_inc(high_made, 1)

                act.sem_inc(high_made, 2)
                for run in runs:
                    lagged(act, run, 0 if quick else 1, bend, no_split if quick else high)
                    if run[2] == sections - 1:
                        act.wait_ge(acc_ready, run[1] + 1)
                        nc.scalar.activation(OT[:, run[1] * HALF:(run[1] + 1) * HALF],
                                             acc[:, :, :].rearrange("p g n -> p (g n)"), ACT.Copy).then_inc(acc_read, 1)

            @block.vector
            def _(dve):
                def gate(i, k, run):
                    j = k // G
                    s = count(i, k, run)
                    if quick:
                        if k % G == 0:
                            dve.wait_ge(bias_ready, unit(i, j, run) + 1)
                        dve.wait_ge(s_ready, s + 1)
                        nc.vector.scalar_tensor_tensor(T1[:, :], pa[k % 2][:, :], BX[:, j, 0:1],
                                                       S[:, k % 2, :], ALU.add, ALU.mult).then_inc(t1_ready, 1)
                        dve.wait_ge(b_ready, s + 1)
                        dve.wait_ge(t1_ready, s + 1)
                        nc.vector.scalar_tensor_tensor(T2[:, k % 2, :], pb[k % 2][:, :], BX[:, j, 2:3],
                                                       T1[:, :], ALU.add, ALU.mult).then_inc(t2_ready, 1)
                    else:
                        dve.wait_ge(s_ready, s + 1)
                        dve.wait_ge(b_ready, s + 1)
                        nc.vector.tensor_tensor(T2[:, k % 2, :], S[:, k % 2, :], pb[k % 2][:, :], ALU.mult).then_inc(t2_ready, 1)
                    dve.wait_ge(t2_ready, s + 1)
                    if quick:
                        dve.wait_ge(summed, s + 1 + WR_FREE)
                    else:
                        dve.wait_ge(high_made, s + 1)
                        dve.wait_ge(low_made, s + 1)
                    nc.vector.tensor_tensor(HF[:, k % 2, :], T2[:, k % 2, :], pg[k % 2][:, :], ALU.mult).then_inc(gated, 1)

                def low(i, k, run):
                    s = count(i, k, run)
                    dve.wait_ge(high_made, s + 3)
                    nc.vector.tensor_tensor(HS[:, k % 2, 1, :], HF[:, k % 2, :], HS[:, k % 2, 0, :].bitcast(F32),
                                            ALU.subtract).then_inc(low_made, 1)

                dve.sem_inc(gated, 2)
                dve.sem_inc(low_made, 2)
                if not quick:
                    nc.vector.memset(zeros[:, :], 0.0).then_inc(opened, 1)
                for run in runs:
                    lagged(dve, run, 0 if quick else 1, gate, no_split if quick else low)


def route_grouped(nc, name, XT, XR, ident, iota, earlier, w_router, b_router, gateT, weights, bias=None):
    E, NG, K, CAP = 64, 8, 8, 256
    EG = E // NG
    FAR = 1e30
    with Stage(nc, name) as st:
        wr = st.sb("wr", [P, E])
        br = st.sb("br", [P, E])
        scores = st.sb("scores", [P, TILES, E])
        biased = st.sb("biased", [P, TILES, E])
        work = st.sb("work", [P, TILES, E])
        best = st.sb("best", [P, TILES, NG])
        second = st.sb("second", [P, TILES, NG])
        ties = st.sb("ties", [P, TILES, NG])
        top = st.sb("top", [P, TILES, 8])
        where = st.sb("where", [P, TILES, 8], U32)
        wheref = st.sb("wheref", [P, TILES, 8])
        gmask = st.sb("gmask", [P, TILES, NG])
        chosen = st.sb("chosen", [P, TILES, E])
        chosen16 = st.sb("chosen16", [P, TILES * E], BF16)
        total = st.sb("total", [P, TILES])
        ahead = st.sb("ahead", [P, TILES, E])
        gates = st.sb("gates", [P, TILES, 2, 96])
        part16 = st.sb("part16", [P, TILES, E], BF16)
        pl = st.ps("pl", [P, TILES, E])
        before = st.ps("before", [P, TILES, E])
        inall = st.ps("inall", [P, TILES, E])
        turned = [st.ps(f"turned{i}", [P, GROUP]) for i in range(2)]
        loaded = st.sem("loaded")
        x_rounded = st.sem("x_rounded")
        logits_ready = st.sem("logits_ready")
        scores_ready = st.sem("scores_ready")
        chosen_ready = st.sem("chosen_ready")
        counted = st.sem("counted")
        gates_ready = st.sem("gates_ready")
        turned_ready = st.sem("turned_ready")
        turned_read = st.sem("turned_read")
        chain = st.sem("chain")
        with nc.Block() as block:
            @block.sync
            def _(sp):
                sp.dma_start(wr[:, :], w_router[:, :]).then_inc(loaded, 16)
                sp.dma_start(br[:, :], b_router.partition_broadcast(P)).then_inc(loaded, 16)
                weights.start_loads(sp)

            @block.gpsimd
            def _(pool):
                split_x(nc, XT, XR, x_rounded, pool, None)
                weights.start_splits(pool, bias)

            @block.tensor
            def _(pe):
                pe.wait_ge(loaded, 32)
                for t in range(TILES):
                    mm = pe.matmul(pl[:, t, :], XT[:, t * P:(t + 1) * P], wr[:, :], start=True, stop=True)
                mm.then_inc(logits_ready, 1)
                pe.wait_ge(chosen_ready, 1)
                for h in range(2):
                    c = slice(h * GROUP, (h + 1) * GROUP)
                    pe.matmul(before[:, :, :].rearrange("p t e -> p (t e)")[:, c], earlier[:, 0, :], chosen16[:, c],
                              start=True, stop=True)
                    mm = pe.matmul(inall[:, :, :].rearrange("p t e -> p (t e)")[:, c], earlier[:, 1, :], chosen16[:, c],
                                   start=True, stop=True)
                mm.then_inc(counted, 1)
                pe.wait_ge(gates_ready, 1)
                for n in range(2 * GROUPS):
                    b, g = n // GROUPS, n % GROUPS
                    if n >= 2:
                        pe.wait_ge(turned_read, n - 1)
                    for t in range(GT):
                        mm = pe.transpose(turned[n % 2][0:96, t * P:(t + 1) * P], gates[:, g * GT + t, b, :], ident[:, :])
                    mm.then_inc(turned_ready, 1)

            @block.scalar
            def _(act):
                split_x(nc, XT, XR, x_rounded, None, act)
                act.wait_ge(logits_ready, 1)
                nc.scalar.activation(scores[:, :, :], pl[:, :, :], ACT.Sigmoid).then_inc(scores_ready, 1)
                for n in range(2 * GROUPS):
                    b, g = n // GROUPS, n % GROUPS
                    act.wait_ge(turned_ready, n + 1)
                    nc.scalar.activation(gateT[:, b, g * GROUP:(g + 1) * GROUP], turned[n % 2][0:96, :],
                                         ACT.Copy).then_inc(turned_read, 1)

            @block.vector
            def _(dve):
                link = Chain(dve, chain)
                v = nc.vector

                def grouped(x):
                    return x[:, :, :].rearrange("p t (g e) -> p (t g) e", e=EG)

                def flat(x):
                    return x[:, :, :].rearrange("p t g -> p (t g)")

                dve.wait_ge(scores_ready, 1)
                dve.wait_ge(loaded, 32)
                link(v.tensor_tensor(biased[:, :, :], scores[:, :, :], br[:, :].unsqueeze(1).broadcast_to([P, TILES, E]), ALU.add))
                link(v.tensor_reduce(flat(best), grouped(biased), AX.X, ALU.max))
                link(v.tensor_tensor(grouped(work), grouped(biased), spread(flat(best), EG), ALU.is_equal))
                link(v.tensor_reduce(flat(ties), grouped(work), AX.X, ALU.add))
                link(v.scalar_tensor_tensor(flat(work), flat(work), -FAR, flat(biased), ALU.mult, ALU.add))
                link(v.tensor_reduce(flat(second), grouped(work), AX.X, ALU.max))
                link(v.tensor_scalar(flat(ties), flat(ties), 2.0, -FAR, ALU.is_lt, ALU.mult))
                link(v.tensor_tensor(flat(ties), flat(ties), flat(best), ALU.add))
                link(v.tensor_tensor(flat(second), flat(second), flat(ties), ALU.max))
                link(v.tensor_tensor(flat(best), flat(best), flat(second), ALU.add))
                for t in range(TILES):
                    m = v.max(top[:, t, :], best[:, t, :])
                link(m)
                for t in range(TILES):
                    m = v.max_index(where[:, t, :], top[:, t, :], best[:, t, :])
                link(m)
                link(v.tensor_copy(wheref[:, :, :], where[:, :, :]))
                link(v.memset(gmask[:, :, :], 0.0))
                for k in range(4):
                    link(v.tensor_tensor(ties[:, :, :], iota[:, 0:NG].unsqueeze(1).broadcast_to([P, TILES, NG]),
                                         spread(wheref[:, :, k], NG), ALU.is_equal))
                    link(v.tensor_tensor(gmask[:, :, :], gmask[:, :, :], ties[:, :, :], ALU.add))
                link(v.tensor_tensor(grouped(biased), grouped(biased), spread(flat(gmask), EG), ALU.mult))
                link(v.tensor_scalar(gmask[:, :, :], gmask[:, :, :], 1.0, FAR, ALU.subtract, ALU.mult))
                link(v.tensor_tensor(grouped(biased), grouped(biased), spread(flat(gmask), EG), ALU.add))
                for t in range(TILES):
                    m = v.max(top[:, t, :], biased[:, t, :])
                link(m)
                for t in range(TILES):
                    m = v.match_replace(work[:, t, :], top[:, t, :], biased[:, t, :], -4.0 * FAR)
                link(m)
                v.tensor_scalar(chosen16[:, :], flat(work), -2.0 * FAR, None, ALU.is_lt).then_inc(chosen_ready, 1)
                link(v.tensor_scalar(flat(chosen), flat(work), -2.0 * FAR, None, ALU.is_lt))
                link(v.tensor_tensor(scores[:, :, :], scores[:, :, :], chosen[:, :, :], ALU.mult))
                link(v.tensor_reduce(total[:, :], scores[:, :, :], AX.X, ALU.add))
                link(v.reciprocal(total[:, :], total[:, :]))
                link(v.tensor_scalar(total[:, :], total[:, :], 2.5, None, ALU.mult))
                link(v.tensor_tensor(scores[:, :, :], scores[:, :, :], spread(total[:, :], E), ALU.mult))
                dve.wait_ge(counted, 1)
                link(v.memset(ahead[:, 0, :], 0.0))
                for t in range(1, TILES):
                    link(v.tensor_tensor(ahead[:, t, :], ahead[:, t - 1, :], inall[:, t - 1, :], ALU.add))
                link(v.tensor_tensor(ahead[:, :, :], ahead[:, :, :], before[:, :, :], ALU.add))
                link(v.tensor_scalar(flat(ahead), flat(ahead), float(CAP), None, ALU.is_lt))
                link(v.tensor_tensor(flat(scores), flat(scores), flat(ahead), ALU.mult))

                def blocks(x):
                    return x[:, :, :].rearrange("p t (b e) -> p t b e", b=2)

                split_gates(nc, link, blocks(scores), [gates[:, :, :, 32 * i:32 * i + 32] for i in range(3)],
                            blocks(part16), blocks(work)).then_inc(gates_ready, 1)


def layer_norm(nc, name, Y, N, C, GB, eps, H=None):
    PARTS = 4
    NT = N // PARTS
    by_act = C >= 256
    with Stage(nc, name) as st:
        square = st.sb("square", [P, N, C])
        mean = st.sb("mean", [P, N])
        var = st.sb("var", [P, N])
        rstd = st.sb("rstd", [P, N])
        centred_ready = st.sem("centred_ready")
        squared = st.sem("squared")
        var_ready = st.sem("var_ready")
        root_ready = st.sem("root_ready")
        scaled = st.sem("scaled")
        chain = st.sem("chain")

        def tiles(g):
            return slice(g * NT, (g + 1) * NT)

        def row(n):
            return GB[:, n, :].unsqueeze(1).broadcast_to([P, NT, C])

        with nc.Block() as block:
            @block.vector
            def _(dve):
                v = nc.vector
                link = Chain(dve, chain)
                for g in range(PARTS):
                    s = tiles(g)
                    link(v.tensor_reduce(mean[:, s], Y[:, s, :], AX.X, ALU.add))
                    link(v.tensor_scalar(mean[:, s], mean[:, s], 1.0 / C, None, ALU.mult))
                    v.tensor_tensor(Y[:, s, :], Y[:, s, :], spread(mean[:, s], C), ALU.subtract).then_inc(centred_ready, 1)
                for g in range(PARTS):
                    s = tiles(g)
                    dve.wait_ge(squared, g + 1)
                    if not by_act:
                        link(v.tensor_reduce(var[:, s], square[:, s, :], AX.X, ALU.add))
                    v.tensor_scalar(var[:, s], var[:, s], 1.0 / C, eps, ALU.mult, ALU.add).then_inc(var_ready, 1)
                for g in range(PARTS):
                    s = tiles(g)
                    dve.wait_ge(root_ready, g + 1)
                    link(v.reciprocal(rstd[:, s], rstd[:, s]))
                    m = v.tensor_tensor(Y[:, s, :], Y[:, s, :], spread(rstd[:, s], C), ALU.mult)
                    if GB is not None:
                        link(m)
                        m = v.tensor_tensor(Y[:, s, :], Y[:, s, :], row(0), ALU.mult)
                        if H is not None:
                            link(m)
                            m = v.tensor_tensor(Y[:, s, :], Y[:, s, :], row(1), ALU.add)
                    m.then_inc(scaled, 1)

            @block.gpsimd
            def _(pool):
                for g in range(PARTS if GB is not None else 0):
                    s = tiles(g)
                    pool.wait_ge(scaled, g + 1)
                    if H is None:
                        nc.gpsimd.tensor_tensor(Y[:, s, :], Y[:, s, :], row(1), ALU.add)
                    else:
                        nc.gpsimd.tensor_tensor(H[:, s, :], H[:, s, :], Y[:, s, :], ALU.add)

            @block.scalar
            def _(act):
                for g in range(PARTS):
                    act.wait_ge(centred_ready, g + 1)
                    if by_act:
                        for t in range(g * NT, (g + 1) * NT):
                            m = nc.scalar.activation(square[:, t, :], Y[:, t, :], ACT.Square, accum_out=var[:, t:t + 1])
                    else:
                        m = nc.scalar.activation(square[:, tiles(g), :], Y[:, tiles(g), :], ACT.Square)
                    m.then_inc(squared, 1)
                for g in range(PARTS):
                    act.wait_ge(var_ready, g + 1)
                    nc.scalar.activation(rstd[:, tiles(g)], var[:, tiles(g)], ACT.Sqrt).then_inc(root_ready, 1)


def choose_tokens(nc, name, H, x, x_rows, w, b, ident, pick):
    BLOCKS, K, CHUNKS = P, 16, 8
    BC = BLOCKS // CHUNKS
    LOW = -3e38
    with Stage(nc, name) as st:
        X = st.sb("X", [P, 4, BC, P])
        W = st.sb("W", [P, P])
        B = st.sb("B", [P, 1])
        prod = st.sb("prod", [P, BC, P])
        scores = st.sb("scores", [P, BLOCKS])
        S = st.sb("S", [P, P])
        S2 = st.sb("S2", [P, P])
        top = st.sb("top", [P, K])
        where = st.sb("where", [P, K], U32)
        row = st.sb("row", [P, K])
        rows = st.sb("rows", [P, K // 2, K])
        index = st.sb("index", [P, TILES], U32)
        turned = st.ps("turned", [P, P])
        spreadrows = st.ps("spreadrows", [P, TILES])
        w_loaded = st.sem("w_loaded")
        x_loaded = [st.sem(f"x_loaded{j}") for j in range(4)]
        scored = st.sem("scored")
        scores_ready = st.sem("scores_ready")
        turned_ready = st.sem("turned_ready")
        rows_ready = st.sem("rows_ready")
        spread_ready = st.sem("spread_ready")
        index_ready = st.sem("index_ready")
        gathered = st.sem("gathered")
        chain = st.sem("chain")
        xb = x.rearrange("s (h p) d -> p (s h) d", p=P)
        with nc.Block() as block:
            @block.sync
            def _(sp):
                sp.dma_start(W[:, :], w[0, :].partition_broadcast(P)).then_inc(w_loaded, 16)
                sp.dma_start(B[:, :], b.partition_broadcast(P)).then_inc(w_loaded, 16)
                for c in range(CHUNKS):
                    if c >= 4:
                        sp.wait_ge(scored, c - 3)
                    sp.dma_start(X[:, c % 4], xb[:, c * BC:(c + 1) * BC, :]).then_inc(x_loaded[c % 4], 16)

            @block.vector
            def _(dve):
                v = nc.vector
                link = Chain(dve, chain)
                dve.wait_ge(w_loaded, 32)
                for c in range(CHUNKS):
                    dve.wait_ge(x_loaded[c % 4], 16 * (c // 4 + 1))
                    v.tensor_tensor(prod[:, :, :], X[:, c % 4], W[:, :].unsqueeze(1).broadcast_to([P, BC, P]),
                                    ALU.mult).then_inc(scored, 1)
                    dve.wait_ge(scored, c + 1)
                    link(v.tensor_reduce(scores[:, c * BC:(c + 1) * BC], prod[:, :, :], AX.X, ALU.add))
                v.tensor_scalar(scores[:, :], scores[:, :], B[:, 0:1], None, ALU.add).then_inc(scores_ready, 1)
                dve.wait_ge(turned_ready, 1)
                link(v.tensor_copy(S[:, :], turned[:, :]))
                link(v.max(top[:, 0:8], S[:, :]))
                link(v.max_index(where[:, 0:8], top[:, 0:8], S[:, :]))
                link(v.match_replace(S2[:, :], top[:, 0:8], S[:, :], LOW))
                link(v.max(top[:, 8:16], S2[:, :]))
                link(v.max_index(where[:, 8:16], top[:, 8:16], S2[:, :]))
                link(v.tensor_copy(row[:, :], where[:, :]))
                link(v.tensor_scalar(row[:, :], row[:, :], pick[:, 8 + TILES:9 + TILES], None, ALU.add))
                v_rows = row[:, :].unsqueeze(1).broadcast_to([P, K // 2, K])
                v.tensor_tensor(rows[:, :, :], v_rows, spread(pick[:, 0:8], K), ALU.mult).then_inc(rows_ready, 1)
                dve.wait_ge(spread_ready, 1)
                v.tensor_copy(index[:, :], spreadrows[:, :]).then_inc(index_ready, 1)

            @block.tensor
            def _(pe):
                pe.wait_ge(scores_ready, 1)
                pe.transpose(turned[:, :], scores[:, :], ident[:, :]).then_inc(turned_ready, 1)
                pe.wait_ge(rows_ready, 1)
                pe.matmul(spreadrows[:, :], rows[:, :, :].rearrange("p a k -> p (a k)"), pick[:, 8:8 + TILES],
                          start=True, stop=True).then_inc(spread_ready, 1)

            @block.gpsimd
            def _(pool):
                pool.wait_ge(index_ready, 1)
                for t in range(TILES):
                    pool.indirect_dma_start(H[:, t, :], None, x_rows,
                                            bass.IndirectOffsetOnAxis(ap=index[:, t:t + 1], axis=0)).then_inc(gathered, 16)
                pool.wait_ge(gathered, 16 * TILES)


def attend(nc, name, H, XT, XN, ident, wq, wk, wv, wo, gamma, beta):
    NH, HD = 8, 16
    with Stage(nc, name) as st:
        WQ = st.sb("WQ", [P, NH, P])
        WK = st.sb("WK", [P, P])
        WV = st.sb("WV", [P, P])
        WO = st.sb("WO", [P, P])
        GB = st.sb("GB", [P, 2, P])
        KT = st.sb("KT", [P, T])
        V = st.sb("V", [P, TILES, P])
        QS = st.sb("QS", [P, NH, P])
        SC = st.sb("SC", [P, NH, L])
        EX = st.sb("EX", [P, NH, L])
        mx = st.sb("mx", [P, NH])
        den = st.sb("den", [P, NH])
        PB = st.sb("PB", [P, NH, P])
        PT = st.sb("PT", [P, NH, P])
        CX = st.sb("CX", [P, P])
        CT = st.sb("CT", [P, P])
        Y = st.sb("Y", [P, TILES, P])
        pq = st.ps("pq", [P, NH, P])
        psc = st.ps("psc", [P, NH, P])
        ppt = st.ps("ppt", [P, NH, P])
        pc = st.ps("pc", [P, P])
        po = st.ps("po", [P, 2, P])
        loaded = st.sem("loaded")
        kv_made = st.sem("kv_made")
        kv_read = st.sem("kv_read")
        q_made = st.sem("q_made")
        q_read = st.sem("q_read")
        sc_made = st.sem("sc_made")
        sc_shifted = st.sem("sc_shifted")
        exp_made = st.sem("exp_made")
        prob_made = st.sem("prob_made")
        pt_made = st.sem("pt_made")
        pt_read = st.sem("pt_read")
        ctx_made = st.sem("ctx_made")
        ctx_read = st.sem("ctx_read")
        ctxt_made = st.sem("ctxt_made")
        ctxt_read = st.sem("ctxt_read")
        o_made = st.sem("o_made")
        o_read = st.sem("o_read")
        sc_a = st.sem("scores_copied")
        sc_b = st.sem("max_made")
        sc_c = st.sem("sum_made")
        sc_d = st.sem("reciprocal_made")
        chain = st.sem("chain")

        def staggered(eng, pieces):
            late = max(lag for _, lag in pieces)

            def turn(base, off):
                for piece, lag in pieces:
                    n = off - lag
                    if not isinstance(base, int) or 0 <= n < TILES:
                        piece(base + n, lambda m, n=n: base * m + n * m)

            for i in range(late):
                turn(0, i)
            with eng.Fori(0, TILES - late) as i:
                turn(i, late)
            for i in range(TILES, TILES + late):
                turn(0, i)

        wide = pq[:, :, :].rearrange("p h c -> p (h c)")
        with nc.Block() as block:
            @block.sync
            def _(sp):
                sp.dma_start(WQ[:, :, :], wq).then_inc(loaded, 16)
                for tile, src in ((WK, wk), (WV, wv), (WO, wo)):
                    sp.dma_start(tile[:, :], src).then_inc(loaded, 16)
                sp.dma_start(GB[:, 0, :], gamma.partition_broadcast(P)).then_inc(loaded, 16)
                sp.dma_start(GB[:, 1, :], beta.partition_broadcast(P)).then_inc(loaded, 16)

            @block.tensor
            def _(pe):
                pe.wait_ge(loaded, 96)
                for g in range(GROUPS):
                    if g >= 2:
                        pe.wait_ge(kv_read, g - 1)
                    pe.matmul(wide[:, g % 2 * GROUP:(g % 2 + 1) * GROUP], WK[:, :], XT[:, g * GROUP:(g + 1) * GROUP],
                              start=True, stop=True).then_inc(kv_made, 1)
                for g in range(GROUPS):
                    pe.wait_ge(kv_read, g + 3)
                    for t in range(GT):
                        i = g * GT + t
                        mm = pe.matmul(pq[:, g % 2 * GT + t, :], XT[:, i * P:(i + 1) * P], WV[:, :], start=True, stop=True)
                    mm.then_inc(kv_made, 1)
                pe.wait_ge(kv_read, 2 * GROUPS)

                def queries(i, at):
                    for h in range(NH):
                        mm = pe.matmul(pq[:, h, :], WQ[:, h, :], XT[:, bass.ds(at(P), P)], start=True, stop=True)
                    mm.then_inc(q_made, 1)

                def scores(i, at):
                    pe.wait_ge(q_read, i + 1)
                    pe.wait_ge(sc_shifted, i + 1)
                    for h in range(NH):
                        mm = pe.matmul(psc[:, h, :], QS[:, h, :], KT[:, bass.ds(at(P), P)], start=True, stop=True)
                    mm.then_inc(sc_made, 1)

                def turn_probs(i, at):
                    pe.wait_ge(prob_made, i + 1)
                    for h in range(NH):
                        mm = pe.transpose(ppt[:, h, :], PB[:, h, :], ident[:, :])
                    mm.then_inc(pt_made, 1)

                def context(i, at):
                    pe.wait_ge(pt_read, i + 1)
                    for h in range(NH):
                        mm = pe.matmul(pc[:, h * HD:(h + 1) * HD], PT[:, h, :],
                                       V[:, bass.ds(i, 1), h * HD:(h + 1) * HD].rearrange("p t c -> p (t c)"),
                                       start=True, stop=True)
                    mm.then_inc(ctx_made, 1)

                def turn_context(i, at):
                    pe.wait_ge(ctx_read, i + 1)
                    pe.wait_ge(o_read, i + 1)
                    pe.transpose(po[:, 0, :], CX[:, :], ident[:, :]).then_inc(ctxt_made, 1)

                def output(i, at):
                    pe.wait_ge(ctxt_read, i + 1)
                    pe.matmul(po[:, 1, :], CT[:, :], WO[:, :], start=True, stop=True).then_inc(o_made, 1)

                staggered(pe, [(queries, 0), (turn_probs, 2), (turn_context, 3), (scores, 0), (output, 3), (context, 2)])

            @block.scalar
            def _(act):
                a = nc.scalar
                for g in range(GROUPS):
                    act.wait_ge(kv_made, g + 1)
                    a.activation(KT[:, g * GROUP:(g + 1) * GROUP], wide[:, g % 2 * GROUP:(g % 2 + 1) * GROUP],
                                 ACT.Copy).then_inc(kv_read, 1)
                for g in range(GROUPS):
                    act.wait_ge(kv_made, GROUPS + g + 1)
                    a.activation(V[:, g * GT:(g + 1) * GT, :], pq[:, g % 2 * GT:(g % 2 + 1) * GT, :],
                                 ACT.Copy).then_inc(kv_read, 1)

                def context(i, at):
                    act.wait_ge(ctx_made, i + 1)
                    a.activation(CX[:, :], pc[:, :], ACT.Copy).then_inc(ctx_read, 1)

                def exps(i, at):
                    act.wait_ge(sc_shifted, i + 2)
                    a.activation(EX[:, :, :], SC[:, :, :], ACT.Exp, scale=HD ** -0.5).then_inc(exp_made, 1)

                def queries(i, at):
                    act.wait_ge(q_made, i + 1)
                    if not isinstance(i, int) or i:
                        act.wait_ge(sc_made, i)
                    a.activation(QS[:, :, :], pq[:, :, :], ACT.Copy).then_inc(q_read, 1)

                def turned_probs(i, at):
                    act.wait_ge(pt_made, i + 1)
                    a.activation(PT[:, :, :], ppt[:, :, :], ACT.Copy).then_inc(pt_read, 1)

                def turned_context(i, at):
                    act.wait_ge(ctxt_made, i + 1)
                    a.activation(CT[:, :], po[:, 0, :], ACT.Copy).then_inc(ctxt_read, 1)

                staggered(act, [(context, 3), (exps, 1), (queries, 0), (turned_probs, 2), (turned_context, 3)])

            @block.vector
            def _(dve):
                v = nc.vector
                link = Chain(dve, chain)
                link(v.memset(PB[:, :, :], 0.0))
                dve.sem_inc(sc_shifted, 1)
                dve.sem_inc(o_read, 1)

                def softmax_first(i, at):
                    dve.wait_ge(sc_made, i + 1)
                    for q in range(QUADS):
                        r = slice(q * L, (q + 1) * L)
                        m = v.tensor_copy(SC[r, :, :], psc[r, :, r])
                    m.then_inc(sc_a, 1)
                    dve.wait_ge(sc_a, i + 1)
                    v.tensor_reduce(mx[:, :], SC[:, :, :], AX.X, ALU.max).then_inc(sc_b, 1)
                    dve.wait_ge(sc_b, i + 1)
                    v.tensor_tensor(SC[:, :, :], SC[:, :, :], spread(mx[:, :], L), ALU.subtract).then_inc(sc_shifted, 1)

                def softmax_second(i, at):
                    dve.wait_ge(exp_made, i + 1)
                    v.tensor_reduce(den[:, :], EX[:, :, :], AX.X, ALU.add).then_inc(sc_c, 1)
                    dve.wait_ge(sc_c, i + 1)
                    v.reciprocal(den[:, :], den[:, :]).then_inc(sc_d, 1)
                    dve.wait_ge(sc_d, i + 1)
                    if not isinstance(i, int) or i:
                        dve.wait_ge(pt_made, i)
                    for q in range(QUADS):
                        r = slice(q * L, (q + 1) * L)
                        m = v.tensor_tensor(PB[r, :, r], EX[r, :, :], spread(den[r, :], L), ALU.mult)
                    m.then_inc(prob_made, 1)

                def output(i, at):
                    dve.wait_ge(o_made, i + 1)
                    t = bass.ds(i, 1)
                    v.tensor_tensor(Y[:, t, :].rearrange("p t c -> p (t c)"), po[:, 1, :],
                                    XN[:, t, :].rearrange("p t c -> p (t c)"), ALU.add).then_inc(o_read, 1)

                staggered(dve, [(softmax_second, 1), (softmax_first, 0), (output, 3)])

        layer_norm(nc, name + "l", Y, TILES, P, GB, 1e-5, H)


def gated_recurrence(nc, name, H, XT, ident, w):
    NH, HK, HV, VI = 4, 16, 32, 16
    VB = 4
    SPLIT = 1536
    with Stage(nc, name) as st:
        OV = st.sb("OV", [P, T])
        WO = st.sb("WO", [P, P])
        WG = st.sb("WG", [P, P])
        with Stage(nc, name + "a") as sa:
            K = sa.sb("K", [P, T])
            Q = sa.sb("Q", [P, T])
            DEC = sa.sb("DEC", [P, T])
            loaded = sa.sem("loaded")
            with Stage(nc, name + "g") as sg:
                WK = sg.sb("WK", [P, P])
                WQ = sg.sb("WQ", [P, P])
                W1 = sg.sb("W1", [P, 16])
                W2 = sg.sb("W2", [16, P])
                B = sg.sb("B", [P, 2])
                MID = sg.sb("MID", [16, T])
                A = sg.sb("A", [P, T])
                R = sg.sb("R", [P, T])
                U = sg.sb("U", [P, T])
                pA = sg.ps("pA", [P, T])
                pB = sg.ps("pB", [P, T])
                kq_made = sg.sem("kq_made")
                kq_read = sg.sem("kq_read")
                mid_made = sg.sem("mid_made")
                mid_read = sg.sem("mid_read")
                z_made = sg.sem("z_made")
                neg_made = sg.sem("neg_made")
                e_made = sg.sem("e_made")
                act_chain = sg.sem("act_chain")
                u_made = sg.sem("u_made")
                ln_made = sg.sem("ln_made")
                sp_made = sg.sem("sp_made")
                dec_made = sg.sem("dec_made")
                chain = sg.sem("chain")
                with nc.Block() as block:
                    @block.sync
                    def _(sp):
                        for tile, src in ((WK, w["Wk"]), (WQ, w["Wq"]), (W1, w["Wgk1"]), (W2, w["Wgk2"]),
                                          (WO, w["Wo"]), (WG, w["Wg"])):
                            sp.dma_start(tile[:, :], src).then_inc(loaded, 16)
                        sp.dma_start(B[:, 0:1], w["bgk2"]).then_inc(loaded, 16)

                    @block.tensor
                    def _(pe):
                        pe.wait_ge(loaded, 112)

                        def project(out, lhsT, rhs, done):
                            for g in range(GROUPS):
                                s = slice(g * GROUP, (g + 1) * GROUP)
                                mm = pe.matmul(out[:, s], lhsT[:, :], rhs[:, s], start=True, stop=True)
                            mm.then_inc(done, 1)

                        project(pA, WK, XT, kq_made)
                        project(pB, WQ, XT, kq_made)
                        pe.wait_ge(kq_read, 2)
                        project(pB[0:16, :], W1, XT, mid_made)
                        pe.wait_ge(mid_read, 1)
                        project(pA, W2, MID, z_made)

                    @block.scalar
                    def _(act):
                        a = nc.scalar
                        act.wait_ge(kq_made, 1)
                        a.activation(K[:, :], pA[:, :], ACT.Copy).then_inc(kq_read, 1)
                        act.wait_ge(kq_made, 2)
                        a.activation(Q[:, :], pB[:, :], ACT.Copy, scale=HK ** -0.5).then_inc(kq_read, 1)
                        act.wait_ge(mid_made, 1)
                        a.activation(MID[:, :], pB[0:16, :], ACT.Copy).then_inc(mid_read, 1)
                        act.wait_ge(z_made, 1)
                        act.wait_ge(neg_made, 1)
                        a.activation(R[:, :], pA[:, :], ACT.Relu, scale=-1.0, bias=B[:, 1:2])
                        a.activation(A[:, :], pA[:, :], ACT.Abs, bias=B[:, 0:1]).then_inc(act_chain, 1)
                        act.wait_ge(act_chain, 1)
                        a.activation(A[:, :], A[:, :], ACT.Exp, scale=-1.0).then_inc(e_made, 1)
                        act.wait_ge(u_made, 1)
                        a.activation(OV[:, :], U[:, :], ACT.Ln).then_inc(ln_made, 1)
                        act.wait_ge(sp_made, 1)
                        a.activation(DEC[:, :], R[:, :], ACT.Exp, scale=-1.0 / 16.0).then_inc(dec_made, 1)

                    @block.vector
                    def _(dve):
                        v = nc.vector
                        link = Chain(dve, chain)
                        dve.wait_ge(loaded, 112)
                        v.tensor_scalar(B[:, 1:2], B[:, 0:1], -1.0, None, ALU.mult).then_inc(neg_made, 1)
                        dve.wait_ge(e_made, 1)
                        v.tensor_scalar(U[:, :], A[:, :], 1.0, None, ALU.add).then_inc(u_made, 1)
                        dve.wait_ge(u_made, 1)
                        link(v.scalar_tensor_tensor(A[:, :], U[:, :], 1.0, A[:, :], ALU.subtract, ALU.subtract))
                        link(v.tensor_tensor(R[:, :], R[:, :], A[:, :], ALU.subtract))
                        dve.wait_ge(ln_made, 1)
                        v.tensor_tensor(R[:, :], R[:, :], OV[:, :], ALU.add).then_inc(sp_made, 1)
                        dve.wait_ge(dec_made, 1)
                        v.memset(DEC[:, 0:T:L], 0.0)

            with Stage(nc, name + "s") as ss:
                W = ss.sb("W", [P, VB, 2 * P])
                zeros = ss.sb("zeros", [P, GROUP], BF16)
                KV = ss.sb("KV", [P, T])
                HS = ss.sb("HS", [P, 2, T])
                QH = ss.sb("QH", [P, 2, T])
                pv = [ss.ps(f"pv{g}", [P, GROUP]) for g in range(GROUPS)]
                acc = ss.ps("acc", [P, GROUPS, GROUP])
                w_loaded = [ss.sem(f"w_loaded{j}") for j in range(VB)]
                zeroed = ss.sem("zeroed")
                v_made = ss.sem("v_made")
                kv_made = ss.sem("kv_made")
                scanned = ss.sem("scanned")
                qh_pool = ss.sem("qh_pool")
                qh_dve = ss.sem("qh_dve")
                summed = ss.sem("summed")
                with nc.Block() as block:
                    @block.sync
                    def _(sp):
                        for j in range(VB):
                            sp.dma_start(W[:, j, :], w["units"][j]).then_inc(w_loaded[j], 16)
                        with sp.Fori(1, VI // VB) as i:
                            for j in range(VB):
                                sp.wait_ge(summed, i * VB + (j + (3 - VB)))
                                sp.dma_start(W[:, j, :], w["units"][bass.ds(i * VB + j, 1)]
                                             .rearrange("u p n -> p (u n)")).then_inc(w_loaded[j], 16)

                    @block.tensor
                    def _(pe):
                        def first(i, j):
                            i, j = (i + 1, j - VB) if j >= VB else (i, j)
                            pe.wait_ge(w_loaded[j], i * 16 + 16)
                            for g in range(GROUPS):
                                pe.wait_ge(kv_made, i * (4 * VB) + (4 * j + g + 1))
                                pe.matmul(pv[g][:, :], W[:, j, 0:P], XT[:, g * GROUP:(g + 1) * GROUP],
                                          start=True, stop=True).then_inc(v_made, 1)

                        def second(i, j):
                            pe.wait_ge(qh_dve, i * VB + (j + 1))
                            pe.wait_ge(qh_pool, i * VB + (j + 3))
                            for g in range(GROUPS):
                                mm = pe.matmul(acc[:, g, :], W[:, j, P:2 * P], QH[:, j % 2, g * GROUP:(g + 1) * GROUP],
                                               start=False, stop=False, skip_group_check=True)
                            mm.then_inc(summed, 1)

                        pe.sem_inc(summed, 2)
                        pe.wait_ge(zeroed, 1)
                        for g in range(GROUPS):
                            pe.matmul(acc[:, g, :], zeros[:, 0:P], zeros[:, :], start=True, stop=False,
                                      skip_group_check=True)
                        first(0, 0)
                        with pe.Fori(0, VI // VB - 1) as i:
                            for j in range(VB):
                                first(i, j + 1)
                                second(i, j)
                        for j in range(VB):
                            if j + 1 < VB:
                                first(VI // VB - 1, j + 1)
                            second(VI // VB - 1, j)

                    @block.vector
                    def _(dve):
                        v = nc.vector
                        v.memset(zeros[:, :], 0.0).then_inc(zeroed, 1)
                        dve.sem_inc(kv_made, 4)
                        with dve.Fori(0, VI // VB) as i:
                            for j in range(VB):
                                for g in range(GROUPS):
                                    c = slice(g * GROUP, (g + 1) * GROUP)
                                    dve.wait_ge(v_made, i * (4 * VB) + (4 * j + g + 1))
                                    v.tensor_tensor(KV[:, c], K[:, c], pv[g][:, :], ALU.mult).then_inc(kv_made, 1)
                                dve.wait_ge(kv_made, i * (4 * VB) + (4 * j + 8))
                                dve.wait_ge(qh_pool, i * VB + (j + 1))
                                v.tensor_tensor_scan(HS[:, j % 2, :], DEC[:, :], KV[:, :], 0.0, ALU.mult,
                                                     ALU.add).then_inc(scanned, 1)
                                dve.wait_ge(scanned, i * VB + (j + 1))
                                dve.wait_ge(summed, i * VB + (j + 1))
                                v.tensor_tensor(QH[:, j % 2, SPLIT:T], HS[:, j % 2, SPLIT:T], Q[:, SPLIT:T],
                                                ALU.mult).then_inc(qh_dve, 1)

                    @block.gpsimd
                    def _(pool):
                        pool.sem_inc(qh_pool, 2)
                        with pool.Fori(0, VI // VB) as i:
                            for j in range(VB):
                                pool.wait_ge(summed, i * VB + (j + 1))
                                pool.wait_ge(scanned, i * VB + (j + 1))
                                nc.gpsimd.tensor_tensor(QH[:, j % 2, 0:SPLIT], HS[:, j % 2, 0:SPLIT], Q[:, 0:SPLIT],
                                                        ALU.mult).then_inc(qh_pool, 1)

                    @block.scalar
                    def _(act):
                        act.wait_ge(summed, VI + 2)
                        nc.scalar.activation(OV[:, :], acc[:, :, :].rearrange("p g n -> p (g n)"), ACT.Copy)

        with Stage(nc, name + "p") as sp_:
            Y = sp_.sb("Y", [P, TILES * NH, HV])
            SG = sp_.sb("SG", [P, TILES, P])
            Yt = Y[:, :, :].rearrange("p (t h) v -> p t (h v)", h=NH)
            tA = sp_.ps("tA", [P, GROUPS, GT, P])
            tB = sp_.ps("tB", [P, GROUPS, GT, P])
            y_turned = sp_.sem("y_turned")
            g_made = sp_.sem("g_made")
            with nc.Block() as block:
                @block.tensor
                def _(pe):
                    for g in range(GROUPS):
                        for t in range(GT):
                            i = g * GT + t
                            mm = pe.transpose(tA[:, g, t, :], OV[:, i * P:(i + 1) * P], ident[:, :])
                        mm.then_inc(y_turned, 1)
                        for t in range(GT):
                            i = g * GT + t
                            mm = pe.matmul(tB[:, g, t, :], XT[:, i * P:(i + 1) * P], WG[:, :], start=True, stop=True)
                        mm.then_inc(g_made, 1)

                @block.scalar
                def _(act):
                    for g in range(GROUPS):
                        act.wait_ge(g_made, g + 1)
                        nc.scalar.activation(SG[:, g * GT:(g + 1) * GT, :], tB[:, g], ACT.Silu)

                @block.vector
                def _(dve):
                    for g in range(GROUPS):
                        dve.wait_ge(y_turned, g + 1)
                        nc.vector.tensor_copy(Yt[:, g * GT:(g + 1) * GT, :], tA[:, g])

            layer_norm(nc, name + "l", Y, TILES * NH, HV, None, 1e-5)
            gated_ready = sp_.sem("gated_ready")
            turned = sp_.sem("turned")
            turned_read = sp_.sem("turned_read")
            out_made = sp_.sem("out_made")
            with nc.Block() as block:
                @block.vector
                def _(dve):
                    for g in range(GROUPS):
                        s = slice(g * GT, (g + 1) * GT)
                        nc.vector.tensor_tensor(SG[:, s, :], SG[:, s, :], Yt[:, s, :], ALU.mult).then_inc(gated_ready, 1)
                    for g in range(GROUPS):
                        s = slice(g * GT, (g + 1) * GT)
                        dve.wait_ge(out_made, g + 1)
                        nc.vector.tensor_tensor(H[:, s, :], H[:, s, :], tB[:, g], ALU.add)

                @block.tensor
                def _(pe):
                    for g in range(GROUPS):
                        pe.wait_ge(gated_ready, g + 1)
                        for t in range(GT):
                            mm = pe.transpose(tA[:, g, t, :], SG[:, g * GT + t, :], ident[:, :])
                        mm.then_inc(turned, 1)
                    for g in range(GROUPS):
                        pe.wait_ge(turned_read, g + 1)
                        for t in range(GT):
                            i = g * GT + t
                            mm = pe.matmul(tB[:, g, t, :], OV[:, i * P:(i + 1) * P], WO[:, :], start=True, stop=True)
                        mm.then_inc(out_made, 1)

                @block.scalar
                def _(act):
                    for g in range(GROUPS):
                        act.wait_ge(turned, g + 1)
                        nc.scalar.activation(OV[:, g * GROUP:(g + 1) * GROUP], tA[:, g].rearrange("p t c -> p (t c)"),
                                             ACT.Copy).then_inc(turned_read, 1)


def turn(nc, name, X, XT, ident):
    with Stage(nc, name) as st:
        turned = st.ps("turned", [P, GROUPS, GROUP])
        turned_ready = st.sem("turned_ready")
        with nc.Block() as block:
            @block.tensor
            def _(pe):
                for g in range(GROUPS):
                    for t in range(GT):
                        mm = pe.transpose(turned[:, g, t * P:(t + 1) * P], X[:, g * GT + t, :], ident[:, :])
                    mm.then_inc(turned_ready, 1)

            @block.scalar
            def _(act):
                for g in range(GROUPS):
                    act.wait_ge(turned_ready, g + 1)
                    nc.scalar.activation(XT[:, g * GROUP:(g + 1) * GROUP], turned[:, g, :], ACT.Copy)


def reach(n, back):
    return (slice(0, L - n), slice(n, L)) if back else (slice(n, L), slice(0, L - n))


def by_sequence(x):
    return x.rearrange("p (b l) -> p b l", l=L)


def mamba_direction(nc, name, XI, YS, ident, selector, w, li, back):
    DS = 16
    with Stage(nc, name) as st:
        XC = st.sb("XC", [P, 2, T])
        DT = st.sb("DT", [P, 2, T])
        DU = st.sb("DU", [P, 2, T])
        BC = st.sb("BC", [96, T], BF16)
        V = st.sb("V", [P, 2, 7])
        AN = st.sb("AN", [P, 2, DS])
        with Stage(nc, name + "p") as sp_:
            diag = sp_.sb("diag", [P, 2, 2, P])
            WBCD = sp_.sb("WBCD", [P, 2, 104])
            WDT = sp_.sb("WDT", [8, 2, P])
            D8 = sp_.sb("D8", [8, T])
            U = sp_.sb("U", [P, 2, T])
            pp = [sp_.ps(f"pp{dh}", [P, GROUPS, GROUP]) for dh in range(2)]
            parts = split_parts(sp_)
            loaded = sp_.sem("loaded")
            diag_made = sp_.sem("diag_made")
            conv_made = sp_.sem("conv_made")
            xc_made = sp_.sem("xc_made")
            far_made = sp_.sem("far_made")
            near_made = sp_.sem("near_made")
            taps_added = sp_.sem("taps_added")
            bcd_made = sp_.sem("bcd_made")
            bc_read = sp_.sem("bc_read")
            d8_read = sp_.sem("d8_read")
            dt_made = sp_.sem("dt_made")
            abs_made = sp_.sem("abs_made")
            e_made = sp_.sem("e_made")
            u_made = sp_.sem("u_made")
            ln_made = sp_.sem("ln_made")
            a_made = sp_.sem("a_made")
            chain = sp_.sem("chain")
            W2 = GROUP * 2

            with nc.Block() as block:
                @block.sync
                def _(sp):
                    for tile, src in ((WBCD, w["bcd"]), (WDT, w["dt"]), (V, w["v"]), (AN, w["a"])):
                        sp.dma_start(tile[:, :, :], src[li, int(back)]).then_inc(loaded, 16)

                @block.vector
                def _(dve):
                    v = nc.vector
                    link = Chain(dve, chain)
                    dve.wait_ge(loaded, 64)
                    for dh in range(2):
                        for n in range(2):
                            v.tensor_scalar(diag[:, dh, n, :], ident[:, :], V[:, dh, 3 - n:4 - n], None,
                                            ALU.mult).then_inc(diag_made, 1)
                    for m in range(2 * GROUPS):
                        g, dh = m // 2, m % 2
                        c = slice(g * GROUP, (g + 1) * GROUP)
                        to, frm = reach(3, back)
                        u3 = by_sequence(U[:, dh, c])[:, :, to]
                        dve.wait_ge(far_made, m + 1)
                        v.scalar_tensor_tensor(u3, by_sequence(XI[:, dh, c])[:, :, frm], V[:, dh, 0:1], u3,
                                               ALU.mult, ALU.add).then_inc(near_made, 1)
                        dve.wait_ge(near_made, m + 1)
                        dve.wait_ge(conv_made, m + 1)
                        v.tensor_tensor(U[:, dh, c], U[:, dh, c], pp[dh][:, g, :], ALU.add).then_inc(taps_added, 1)
                    for g in range(GROUPS):
                        dve.wait_ge(bcd_made, g + 1)
                        split(nc, link, parts, pp[0][0:96, g, :], BC[:, g * GROUP:(g + 1) * GROUP])
                        dve.sem_inc(bc_read, 1)
                    dve.wait_ge(a_made, 1)
                    link(v.tensor_scalar(AN[:, :, :], AN[:, :, :], -1.0, None, ALU.mult))
                    for n in range(4):
                        dh, c = 1 - n // 2, slice(n % 2 * W2, (n % 2 + 1) * W2)
                        dve.wait_ge(e_made, n + 1)
                        link(v.tensor_scalar(U[:, dh, c], DU[:, dh, c], 1.0, None, ALU.add))
                        link(v.scalar_tensor_tensor(DU[:, dh, c], U[:, dh, c], 1.0, DU[:, dh, c], ALU.subtract, ALU.subtract))
                        dve.sem_inc(u_made, 1)
                        link(v.tensor_tensor(DT[:, dh, c], DT[:, dh, c], DU[:, dh, c], ALU.subtract))
                    for n in range(4):
                        dh, c = 1 - n // 2, slice(n % 2 * W2, (n % 2 + 1) * W2)
                        dve.wait_ge(ln_made, n + 1)
                        link(v.tensor_tensor(DT[:, dh, c], DT[:, dh, c], U[:, dh, c], ALU.add))
                        v.tensor_tensor(DU[:, dh, c], DT[:, dh, c], XC[:, dh, c], ALU.mult)

                @block.gpsimd
                def _(pool):
                    pool.wait_ge(loaded, 64)
                    to, frm = reach(2, back)
                    rim = slice(L - 2, L) if back else slice(0, 2)
                    for m in range(2 * GROUPS):
                        g, dh = m // 2, m % 2
                        u = by_sequence(U[:, dh, g * GROUP:(g + 1) * GROUP])
                        nc.gpsimd.memset(u[:, :, rim], 0.0)
                        nc.gpsimd.tensor_scalar(u[:, :, to], by_sequence(XI[:, dh, g * GROUP:(g + 1) * GROUP])[:, :, frm],
                                                V[:, dh, 1:2], None, ALU.mult).then_inc(far_made, 1)

                @block.tensor
                def _(pe):
                    pe.wait_ge(diag_made, 4)
                    to, frm = reach(1, back)
                    for m in range(2 * GROUPS):
                        g, dh = m // 2, m % 2
                        x = by_sequence(XI[:, dh, g * GROUP:(g + 1) * GROUP])
                        out = by_sequence(pp[dh][:, g, :])
                        pe.matmul(out, diag[:, dh, 0, :], x, start=True, stop=False, skip_group_check=True)
                        pe.matmul(out[:, :, to], diag[:, dh, 1, :], x[:, :, frm], start=False, stop=True,
                                  skip_group_check=True).then_inc(conv_made, 1)
                    for g in range(GROUPS):
                        pe.wait_ge(xc_made, 2 * g + 2)
                        for dh in range(2):
                            mm = pe.matmul(pp[0][0:104, g, :], WBCD[:, dh, :], XC[:, dh, g * GROUP:(g + 1) * GROUP],
                                           start=(dh == 0), stop=(dh == 1))
                        mm.then_inc(bcd_made, 1)
                    for dh in (1, 0):
                        for g in range(GROUPS):
                            pe.wait_ge(d8_read, g + 1)
                            if dh == 0:
                                pe.wait_ge(bc_read, g + 1)
                            pe.matmul(pp[dh][:, g, :], WDT[:, dh, :], D8[:, g * GROUP:(g + 1) * GROUP],
                                      start=True, stop=True).then_inc(dt_made, 1)

                @block.scalar
                def _(act):
                    a = nc.scalar
                    act.wait_ge(loaded, 64)
                    for g in range(GROUPS):
                        for dh in range(2):
                            act.wait_ge(taps_added, 2 * g + dh + 1)
                            a.activation(XC[:, dh, g * GROUP:(g + 1) * GROUP], U[:, dh, g * GROUP:(g + 1) * GROUP], ACT.Silu,
                                         bias=V[:, dh, 4:5]).then_inc(xc_made, 1)
                    for g in range(GROUPS):
                        act.wait_ge(bcd_made, g + 1)
                        a.activation(D8[:, g * GROUP:(g + 1) * GROUP], pp[0][96:104, g, :], ACT.Copy).then_inc(d8_read, 1)
                    a.activation(AN[:, :, :], AN[:, :, :], ACT.Exp).then_inc(a_made, 1)
                    for n in range(4):
                        dh, m = 1 - n // 2, n % 2
                        c = slice(m * W2, (m + 1) * W2)
                        z = pp[dh][:, 2 * m:2 * m + 2, :].rearrange("p g n -> p (g n)")
                        act.wait_ge(dt_made, n // 2 * GROUPS + 2 * m + 2)
                        a.activation(DT[:, dh, c], z, ACT.Relu, bias=V[:, dh, 5:6])
                        a.activation(DU[:, dh, c], z, ACT.Abs, bias=V[:, dh, 5:6]).then_inc(abs_made, 1)
                        act.wait_ge(abs_made, n + 1)
                        a.activation(DU[:, dh, c], DU[:, dh, c], ACT.Exp, scale=-1.0).then_inc(e_made, 1)
                    for n in range(4):
                        dh, c = 1 - n // 2, slice(n % 2 * W2, (n % 2 + 1) * W2)
                        act.wait_ge(u_made, n + 1)
                        a.activation(U[:, dh, c], U[:, dh, c], ACT.Ln).then_inc(ln_made, 1)

        N = DS
        with Stage(nc, name + "s") as ss:
            DA = ss.sb("DA", [P, 2, HALF])
            DBU = ss.sb("DBU", [P, 2, HALF])
            HS = ss.sb("HS", [P, 4, HALF])
            HC = ss.sb("HC", [P, 4, HALF])
            CB = ss.sb("CB", [P, 2, HALF])
            AJ = ss.sb("AJ", [P, 2, 2])
            AC = ss.sb("AC", [P, 2, HALF])
            zeros = ss.sb("zeros", [P, GROUP], BF16)
            pb = ss.ps("pb", [P, HALF])
            pc = ss.ps("pc", [P, HALF])
            acc = [ss.ps(f"acc{dh}", [P, HALF]) for dh in range(2)]
            zeroed = ss.sem("zeroed")
            b_made = ss.sem("b_made")
            c_made = ss.sem("c_made")
            c_copied = ss.sem("c_copied")
            a_copied = ss.sem("a_copied")
            da_made = ss.sem("da_made")
            multiplied = ss.sem("multiplied")
            scanned = ss.sem("scanned")
            hc_made = ss.sem("hc_made")
            summed = ss.sem("summed")
            acc_read = ss.sem("acc_read")
            chain = ss.sem("chain")
            step = -1 if back else 1
            first_token = L - 1 if back else 0
            rest = slice(0, L - 1) if back else slice(1, L)

            with nc.Block() as block:
                @block.tensor
                def _(pe):
                    def spread_bc(i, u, th):
                        i, u = (i + 1, u - 2) if u >= 2 else (i, u)
                        m = i * 2 + (th * N + u)
                        pe.wait_ge(multiplied, i * 4 + (2 * (th * N + u) + 2))
                        for g in range(2):
                            mm = pe.matmul(pb[:, g * GROUP:(g + 1) * GROUP],
                                           selector[:, bass.ds(i * 2 + u, 1), :].rearrange("r a c -> r (a c)"),
                                           BC[:, th * HALF + g * GROUP:th * HALF + (g + 1) * GROUP], start=True, stop=True)
                        mm.then_inc(b_made, 1)
                        pe.wait_ge(c_copied, m + 1)
                        for g in range(2):
                            mm = pe.matmul(pc[:, g * GROUP:(g + 1) * GROUP],
                                           selector[:, bass.ds(i * 2 + (N + u), 1), :].rearrange("r a c -> r (a c)"),
                                           BC[:, th * HALF + g * GROUP:th * HALF + (g + 1) * GROUP], start=True, stop=True)
                        mm.then_inc(c_made, 1)

                    def add_up(i, u, th):
                        for dh in range(2):
                            pe.wait_ge(hc_made, i * 4 + (2 * (th * N + u) + dh + 5))
                            for g in range(2):
                                mm = pe.matmul(acc[dh][:, g * GROUP:(g + 1) * GROUP], ident[:, :],
                                               HC[:, 2 * u + dh, g * GROUP:(g + 1) * GROUP], start=False, stop=False,
                                               skip_group_check=True)
                            mm.then_inc(summed, 1)

                    def open_sums():
                        for dh in range(2):
                            for g in range(2):
                                pe.matmul(acc[dh][:, g * GROUP:(g + 1) * GROUP], zeros[:, 0:P], zeros[:, :],
                                          start=True, stop=False, skip_group_check=True)

                    pe.sem_inc(summed, 4)
                    pe.wait_ge(zeroed, 1)
                    open_sums()
                    for u in range(2):
                        spread_bc(0, u, 0)
                    for th in range(2):
                        with pe.Fori(0, N // 2 - 1) as i:
                            for u in range(2):
                                spread_bc(i, u + 2, th)
                                add_up(i, u, th)
                        for u in range(2):
                            add_up(N // 2 - 1, u, th)
                            if th == 0:
                                spread_bc(0, u, 1)
                        if th == 0:
                            pe.wait_ge(acc_read, 1)
                            open_sums()

                @block.scalar
                def _(act):
                    a = nc.scalar
                    act.sem_inc(c_copied, 1)
                    act.wait_ge(zeroed, 2)

                    def decays(i, u, th):
                        a.activation(AJ[:, u, :], AN[:, :, bass.ds(i * 2 + u, 1)].rearrange("p h n -> p (h n)"),
                                     ACT.Copy).then_inc(a_copied, 1)
                        act.wait_ge(a_copied, i * 2 + (th * N + u + 1))
                        for dh in range(2):
                            act.wait_ge(scanned, i * 4 + (2 * (th * N + u) + dh + 1))
                            da = by_sequence(DA[:, dh, :])
                            dt = by_sequence(DT[:, dh, th * HALF:(th + 1) * HALF])
                            a.activation(da[:, :, rest], dt[:, :, rest], ACT.Exp,
                                         scale=AJ[:, u, dh:dh + 1]).then_inc(da_made, 1)

                    def copy_c(i, u, th):
                        act.wait_ge(c_made, i * 2 + (th * N + u + 1))
                        act.wait_ge(hc_made, i * 4 + (2 * (th * N + u) + 2))
                        a.activation(CB[:, u, :], pc[:, :], ACT.Copy).then_inc(c_copied, 1)

                    with act.Fori(0, N // 2) as i:
                        for u in range(2):
                            decays(i, u, 0)
                            copy_c(i, u, 0)
                    decays(0, 0, 1)
                    copy_c(0, 0, 1)
                    decays(0, 1, 1)
                    act.wait_ge(summed, 2 * N + 4)
                    for dh in range(2):
                        m = a.activation(AC[:, dh, :], acc[dh][:, :], ACT.Copy)
                    m.then_inc(acc_read, 1)
                    copy_c(0, 1, 1)
                    with act.Fori(1, N // 2) as i:
                        for u in range(2):
                            decays(i, u, 1)
                            copy_c(i, u, 1)

                @block.vector
                def _(dve):
                    v = nc.vector
                    link = Chain(dve, chain)
                    v.memset(zeros[:, :], 0.0).then_inc(zeroed, 1)
                    for dh in range(2):
                        m = v.memset(DA[:, dh, first_token:HALF:L], 0.0)
                    m.then_inc(zeroed, 1)
                    dve.sem_inc(multiplied, 2)
                    dve.sem_inc(scanned, 2)
                    for th in range(2):
                        tok = slice(th * HALF, (th + 1) * HALF)
                        with dve.Fori(0, N // 2) as i:
                            for u in range(2):
                                dve.wait_ge(b_made, i * 2 + (th * N + u + 1))
                                for dh in range(2):
                                    dve.wait_ge(scanned, i * 4 + (2 * (th * N + u) + dh + 1))
                                    v.tensor_tensor(DBU[:, dh, :], DU[:, dh, tok], pb[:, :], ALU.mult).then_inc(multiplied, 1)
                                for dh in range(2):
                                    s0 = 2 * (th * N + u) + dh
                                    dve.wait_ge(multiplied, i * 4 + (s0 + 3))
                                    dve.wait_ge(da_made, i * 4 + (s0 + 1))
                                    dve.wait_ge(hc_made, i * 4 + (s0 + 1))
                                    v.tensor_tensor_scan(HS[:, 2 * u + dh, ::step], DA[:, dh, ::step], DBU[:, dh, ::step], 0.0,
                                                         ALU.mult, ALU.add).then_inc(scanned, 1)
                    for dh in range(2):
                        if back:
                            m = v.scalar_tensor_tensor(YS[:, dh, :], XC[:, dh, :], V[:, dh, 6:7], YS[:, dh, :],
                                                       ALU.mult, ALU.add)
                        else:
                            m = v.tensor_scalar(YS[:, dh, :], XC[:, dh, :], V[:, dh, 6:7], None, ALU.mult)
                    link(m)
                    dve.wait_ge(acc_read, 1)
                    for dh in range(2):
                        v.tensor_tensor(YS[:, dh, 0:HALF], YS[:, dh, 0:HALF], AC[:, dh, :], ALU.add)
                    dve.wait_ge(summed, 2 * 2 * N + 4)
                    for dh in range(2):
                        v.tensor_tensor(YS[:, dh, HALF:T], YS[:, dh, HALF:T], acc[dh][:, :], ALU.add)

                @block.gpsimd
                def _(pool):
                    pool.sem_inc(hc_made, 4)
                    for th in range(2):
                        with pool.Fori(0, N // 2) as i:
                            for u in range(2):
                                pool.wait_ge(c_copied, i * 2 + (th * N + u + 2))
                                for dh in range(2):
                                    s0 = 2 * (th * N + u) + dh
                                    pool.wait_ge(scanned, i * 4 + (s0 + 3))
                                    pool.wait_ge(summed, i * 4 + (s0 + 1))
                                    nc.gpsimd.tensor_tensor(HC[:, 2 * u + dh, :], HS[:, 2 * u + dh, :], CB[:, u, :],
                                                            ALU.mult).then_inc(hc_made, 1)


def bimamba_layers(nc, name, H, XT, AT, ident, selector, w):
    for layer, li in enumerate((0, 2)):
        with Stage(nc, f"{name}{layer}") as st:
            SZ = st.sb("SZ", [P, 2, T])
            YS = st.sb("YS", [P, 2, T])
            XI = st.sb("XI", [P, 2, T])
            with Stage(nc, f"{name}{layer}i") as si:
                WI = si.sb("WI", [P, 4, P])
                pp = [si.ps(f"pp{i}", [P, HALF]) for i in range(4)]
                loaded = si.sem("loaded")
                made = si.sem("made")
                read = si.sem("read")
                with nc.Block() as block:
                    @block.sync
                    def _(sp):
                        sp.dma_start(WI[:, :, :], w["in"][li]).then_inc(loaded, 16)

                    @block.tensor
                    def _(pe):
                        pe.wait_ge(loaded, 16)
                        for n in range(8):
                            c, th = n // 2, n % 2
                            if n >= 4:
                                pe.wait_ge(read, n - 3)
                            for g in range(2):
                                mm = pe.matmul(pp[n % 4][:, g * GROUP:(g + 1) * GROUP], WI[:, c, :],
                                               XT[:, th * HALF + g * GROUP:th * HALF + (g + 1) * GROUP],
                                               start=True, stop=True)
                            mm.then_inc(made, 1)

                    @block.scalar
                    def _(act):
                        for n in range(8):
                            c, tok = n // 2, slice(n % 2 * HALF, (n % 2 + 1) * HALF)
                            act.wait_ge(made, n + 1)
                            dst, f = (XI[:, c, tok], ACT.Copy) if c < 2 else (SZ[:, c - 2, tok], ACT.Silu)
                            nc.scalar.activation(dst, pp[n % 4][:, :], f).then_inc(read, 1)

            for back in (False, True):
                mamba_direction(nc, f"{name}{layer}{'b' if back else 'f'}", XI, YS, ident, selector, w, li, back)

            with Stage(nc, f"{name}{layer}o") as so:
                WO = so.sb("WO", [P, 2, P])
                GB = so.sb("GB", [P, 2, P])
                AO = so.sb("AO", [P, TILES, P])
                po = so.ps("po", [P, TILES, P])
                loaded = so.sem("loaded")
                gated = so.sem("gated")
                out_made = so.sem("out_made")
                with nc.Block() as block:
                    @block.sync
                    def _(sp):
                        sp.dma_start(WO[:, :, :], w["out"][li]).then_inc(loaded, 16)
                        for n in range(2):
                            sp.dma_start(GB[:, n, :], w["ln"][li, n].partition_broadcast(P)).then_inc(loaded, 16)
                        sp.wait_ge(loaded, 48)

                    @block.vector
                    def _(dve):
                        for g in range(GROUPS):
                            c = slice(g * GROUP, (g + 1) * GROUP)
                            nc.vector.tensor_tensor(YS[:, :, c], YS[:, :, c], SZ[:, :, c], ALU.mult).then_inc(gated, 1)

                    @block.tensor
                    def _(pe):
                        pe.wait_ge(loaded, 48)
                        for g in range(GROUPS):
                            pe.wait_ge(gated, g + 1)
                            for t in range(g * GT, (g + 1) * GT):
                                for dh in range(2):
                                    mm = pe.matmul(po[:, t, :], YS[:, dh, t * P:(t + 1) * P], WO[:, dh, :],
                                                   start=(dh == 0), stop=(dh == 1))
                            mm.then_inc(out_made, 1)

                    @block.scalar
                    def _(act):
                        for g in range(GROUPS):
                            s = slice(g * GT, (g + 1) * GT)
                            act.wait_ge(out_made, g + 1)
                            nc.scalar.activation(AO[:, s, :], po[:, s, :], ACT.Copy)

                layer_norm(nc, f"{name}{layer}l", AO, TILES, P, GB, 1e-6, AT)
            if layer == 0:
                turn(nc, f"{name}{layer}t", AT, XT, ident)
        recycle(nc)
    with nc.Block() as block:
        @block.vector
        def _(dve):
            nc.vector.tensor_tensor(H[:, :, :], H[:, :, :], AT[:, :, :], ALU.add)


def turn_256(nc, name, X, OUT, ident, gate=None):
    with Stage(nc, name) as st:
        turned = st.ps("turned", [P, 2, T])
        turned_ready = st.sem("turned_ready")
        with nc.Block() as block:
            @block.tensor
            def _(pe):
                for k in range(2):
                    for g in range(GROUPS):
                        for t in range(g * GT, (g + 1) * GT):
                            mm = pe.transpose(turned[:, k, t * P:(t + 1) * P], X[:, t, k * P:(k + 1) * P], ident[:, :])
                        mm.then_inc(turned_ready, 1)

            @block.scalar
            def _(act):
                for n in range(2 * GROUPS):
                    k, c = n // GROUPS, slice(n % GROUPS * GROUP, (n % GROUPS + 1) * GROUP)
                    act.wait_ge(turned_ready, n + 1)
                    nc.scalar.activation(OUT[:, k, c], turned[:, k, c], ACT.Copy)
                if gate is not None:
                    nc.scalar.activation(gate[:, :, :], X[:, :, :], ACT.Silu)


def mamba2_direction(nc, name, HT, OU, MS, ident, consts, w, d, back):
    NH, HD, CH = 8, 64, 6
    with Stage(nc, name) as st:
        XBC = st.sb("XBC", [P, CH, T])
        PM = st.sb("PM", [P, TILES, NH * L])
        DD = st.sb("DD", [P, 4, 5])
        DD2 = st.sb("DD2", [P, 2, 5])
        WO = st.sb("WO", [P, 4, 256])
        NW = st.sb("NW", [P, 4])
        SKIP = st.sb("SKIP", [P, 512])

        with Stage(nc, name + "c") as sc:
            WX = sc.sb("WX", [P, 2, CH * P])
            CV = sc.sb("CV", [P, 4, GROUP])
            WT = sc.sb("WT", [P, 2, NH])
            DB = sc.sb("DB", [P, 2, NH])
            Z = sc.sb("Z", [P, TILES * NH])
            A = sc.sb("A", [P, TILES * NH])
            R = sc.sb("R", [P, TILES * NH])
            U = sc.sb("U", [P, TILES * NH])
            LN = sc.sb("LN", [P, TILES * NH])
            RH = sc.sb("RH", [P, TILES * NH, L])
            pp = [sc.ps(f"pp{i}", [P, GROUP]) for i in range(4)]
            pdt = sc.ps("pdt", [P, TILES * NH])
            pd = [sc.ps(f"pd{i}", [P, GROUP]) for i in range(2)]
            wx_loaded = sc.sem("wx_loaded")
            loaded = sc.sem("loaded")
            made = sc.sem("made")
            own_made = sc.sem("own_made")
            conv_made = sc.sem("conv_made")
            cv_read = sc.sem("cv_read")
            dt_made = sc.sem("dt_made")
            z_made = sc.sem("z_made")
            e_made = sc.sem("e_made")
            act_chain = sc.sem("act_chain")
            u_made = sc.sem("u_made")
            ln_made = sc.sem("ln_made")
            da_made = sc.sem("da_made")
            alog_bounded = sc.sem("alog_bounded")
            dec_made = sc.sem("dec_made")
            masked = sc.sem("masked")
            rh_made = sc.sem("rh_made")
            spread_made = sc.sem("spread_made")
            decay_scanned = sc.sem("decay_scanned")
            chain = sc.sem("chain")
            first_token = L - 1 if back else 0
            step = -1 if back else 1
            UNITS = [(c, g) for c in range(CH) for g in range(GROUPS)]
            FLAT = PM[:, :, :].rearrange("p t c -> p (t c)")
            BLOCKS = PM[:, :, :].rearrange("p t (h l) -> p (t h) l", l=L)

            def per_head(row):
                return DB[:, row, :].unsqueeze(1).broadcast_to([P, TILES, NH])

            def heads(x):
                return x[:, :].rearrange("p (t h) -> p t h", h=NH)

            def taps(c):
                return DD[:, c, :] if c < 4 else DD2[:, c - 4, :]

            with nc.Block() as block:
                @block.sync
                def _(sp):
                    sp.dma_start(WT[:, :, :], w["wt"][d]).then_inc(loaded, 16)
                    for n in range(2):
                        sp.dma_start(DB[:, n, :], w["db"][d, n].partition_broadcast(P)).then_inc(loaded, 16)
                    sp.dma_start(DD[:, :, :], w["v"][d][:, 0:4, :]).then_inc(loaded, 16)
                    sp.dma_start(DD2[:, :, :], w["v"][d][:, 4:6, :]).then_inc(loaded, 16)
                    sp.dma_start(WX[:, :, :], w["wx"][d]).then_inc(wx_loaded, 16)
                    sp.dma_start(WO[:, :, :], w["wo"][d]).then_inc(wx_loaded, 16)
                    sp.dma_start(NW[:, :], w["nw"][d]).then_inc(wx_loaded, 16)
                    sp.dma_start(SKIP[:, :], w["skip"][d].partition_broadcast(P)).then_inc(wx_loaded, 16)

                @block.tensor
                def _(pe):
                    pe.wait_ge(loaded, 80)
                    for t in range(TILES):
                        for k in range(2):
                            mm = pe.matmul(pdt[:, t * NH:(t + 1) * NH], HT[:, k, t * P:(t + 1) * P], WT[:, k, :],
                                           start=(k == 0), stop=(k == 1))
                    mm.then_inc(dt_made, 1)
                    pe.wait_ge(wx_loaded, 64)
                    for n, (c, g) in enumerate(UNITS):
                        if 12 <= n < 20:
                            m = n - 12
                            pe.wait_ge(rh_made, m // 4 + 1)
                            if m >= 2:
                                pe.wait_ge(decay_scanned, m - 1)
                            pe.matmul(pd[m % 2][:, :], consts["blocks"][:, :],
                                      RH[:, m * 16:(m + 1) * 16, :].rearrange("p a l -> p (a l)"),
                                      start=True, stop=True).then_inc(spread_made, 1)
                        if n >= 4:
                            pe.wait_ge(conv_made, n - 3)
                        for k in range(2):
                            mm = pe.matmul(pp[n % 4][:, :], WX[:, k, c * P:(c + 1) * P],
                                           HT[:, k, g * GROUP:(g + 1) * GROUP], start=(k == 0), stop=(k == 1))
                        mm.then_inc(made, 1)

                @block.scalar
                def _(act):
                    a = nc.scalar
                    for n in range(len(UNITS) + 2):
                        if n == 0:
                            act.wait_ge(alog_bounded, 1)
                            a.activation(DB[:, 1, :], DB[:, 1, :], ACT.Exp).then_inc(act_chain, 1)
                        if n == 1:
                            act.wait_ge(z_made, 1)
                            a.activation(R[:, :], Z[:, :], ACT.Relu)
                            a.activation(A[:, :], Z[:, :], ACT.Abs).then_inc(act_chain, 1)
                            act.wait_ge(act_chain, 2)
                            a.activation(A[:, :], A[:, :], ACT.Exp, scale=-1.0).then_inc(e_made, 1)
                        if n == 3:
                            act.wait_ge(u_made, 1)
                            a.activation(LN[:, :], U[:, :], ACT.Ln).then_inc(ln_made, 1)
                        if n == 5:
                            act.wait_ge(da_made, 1)
                            a.activation(Z[:, :], Z[:, :], ACT.Exp, scale=-1.0).then_inc(dec_made, 1)
                        if n < len(UNITS):
                            act.wait_ge(made, n + 1)
                            if n >= 4:
                                act.wait_ge(cv_read, n - 3)
                            a.activation(CV[:, n % 4, :], pp[n % 4][:, :], ACT.Identity,
                                         scale=taps(UNITS[n][0])[:, 3:4]).then_inc(own_made, 1)
                        if n >= 2:
                            c, g = UNITS[n - 2]
                            act.wait_ge(conv_made, n - 1)
                            a.activation(XBC[:, c, g * GROUP:(g + 1) * GROUP], CV[:, (n - 2) % 4, :], ACT.Silu,
                                         bias=taps(c)[:, 4:5]).then_inc(cv_read, 1)

                @block.vector
                def _(dve):
                    v = nc.vector
                    link = Chain(dve, chain)
                    dve.wait_ge(loaded, 80)
                    v.tensor_scalar(DB[:, 1, :], DB[:, 1, :], 80.0, None, ALU.min).then_inc(alog_bounded, 1)
                    dve.wait_ge(dt_made, 1)
                    v.tensor_tensor(heads(Z), heads(pdt), per_head(0), ALU.add).then_inc(z_made, 1)
                    for n, (c, g) in enumerate(UNITS):
                        if n == 2:
                            dve.wait_ge(e_made, 1)
                            v.tensor_scalar(U[:, :], A[:, :], 1.0, None, ALU.add).then_inc(u_made, 1)
                            dve.wait_ge(u_made, 1)
                            link(v.scalar_tensor_tensor(A[:, :], U[:, :], 1.0, A[:, :], ALU.subtract, ALU.subtract))
                            link(v.tensor_tensor(R[:, :], R[:, :], A[:, :], ALU.subtract))
                        if n == 4:
                            dve.wait_ge(ln_made, 1)
                            link(v.tensor_tensor(R[:, :], R[:, :], LN[:, :], ALU.add))
                            dve.wait_ge(act_chain, 1)
                            v.tensor_tensor(heads(Z), heads(R), per_head(1), ALU.mult).then_inc(da_made, 1)
                        if 13 <= n < 21:
                            m = n - 13
                            dve.wait_ge(spread_made, m + 1)
                            v.tensor_tensor_scan(FLAT[:, m * GROUP:(m + 1) * GROUP][:, ::step], pd[m % 2][:, ::step],
                                                 consts["own"][:, ::step], 0.0, ALU.mult, ALU.add).then_inc(decay_scanned, 1)
                        if 20 <= n:
                            s = slice(64 + (n - 20) * 16, 64 + (n - 19) * 16)
                            dve.wait_ge(decay_scanned, 8)
                            v.tensor_tensor(BLOCKS[:, s, :], BLOCKS[:, s, :], spread(R[:, s], L), ALU.mult)
                        dve.wait_ge(own_made, n + 1)
                        src, dst = by_sequence(pp[n % 4][:, :]), by_sequence(CV[:, n % 4, :])
                        for k in (1, 2, 3):
                            near, far = reach(k, back)
                            m = v.scalar_tensor_tensor(dst[:, :, near], src[:, :, far], taps(c)[:, 3 - k:4 - k],
                                                       dst[:, :, near], ALU.mult, ALU.add)
                            if k < 3:
                                link(m)
                        m.then_inc(conv_made, 1)

                @block.gpsimd
                def _(pool):
                    g = nc.gpsimd
                    pool.wait_ge(wx_loaded, 64)
                    pool.wait_ge(loaded, 80)
                    for c in range(4):
                        g.tensor_scalar(WO[:, c, :], WO[:, c, :], NW[:, c:c + 1], None, ALU.mult)
                    pool.wait_ge(dec_made, 1)
                    for h in range(2):
                        s = slice(h * 64, (h + 1) * 64)
                        mask = consts["own"][:, 0:L].unsqueeze(1).broadcast_to([P, 64, L])
                        g.tensor_tensor(RH[:, s, :], spread(Z[:, s], L), mask, ALU.mult).then_inc(masked, 1)
                        pool.wait_ge(masked, h + 1)
                        g.memset(RH[:, s, first_token:first_token + 1], 0.0).then_inc(rh_made, 1)
                    pool.wait_ge(decay_scanned, 4)
                    g.tensor_tensor(BLOCKS[:, 0:64, :], BLOCKS[:, 0:64, :], spread(R[:, 0:64], L), ALU.mult)

        with Stage(nc, name + "t") as stt:
            WZ = stt.sb("WZ", [P, 2, 512])
            XF = stt.sb("XF", [P, 2, CH, P])
            HF = stt.sb("HF", [P, 2, 2, P])
            XK = stt.sb("XK", [P, 2, 512])
            SZ = stt.sb("SZ", [P, 2, 512])
            M = stt.sb("M", [P, 2, NH, P])
            XD = stt.sb("XD", [P, 512])
            YG = stt.sb("YG", [P, 2, 512])
            SQ = stt.sb("SQ", [P, 512])
            YT = stt.sb("YT", [P, 512])
            MSJ = stt.sb("MSJ", [P, 2])
            pz = stt.ps("pz", [P, 512])
            pcb = stt.ps("pcb", [P, P])
            pxt = stt.ps("pxt", [P, 512])
            py = [stt.ps(f"py{i}", [P, 512]) for i in range(2)]
            pyt = stt.ps("pyt", [P, 512])
            po = stt.ps("po", [P, 256])
            loaded = stt.sem("loaded")
            m_zeroed = stt.sem("m_zeroed")
            copied = stt.sem("copied")
            z_made = stt.sem("z_made")
            cb_made = stt.sem("cb_made")
            xt_made = stt.sem("xt_made")
            sz_made = stt.sem("sz_made")
            xt_read = stt.sem("xt_read")
            m_made = stt.sem("m_made")
            skipped = stt.sem("skipped")
            y_summed = stt.sem("y_summed")
            y_made = stt.sem("y_made")
            yg_made = stt.sem("yg_made")
            sq_made = stt.sem("sq_made")
            yt_made = stt.sem("yt_made")
            yt_read = stt.sem("yt_read")
            out_made = stt.sem("out_made")
            ou_made = stt.sem("ou_made")
            ms_made = stt.sem("ms_made")

            def pipeline(eng, body, order):
                late = max(lag for _, lag in order)
                for i in range(late + late % 2):
                    for piece, lag in order:
                        if i - lag >= 0:
                            body(piece, i - lag, (i - lag) % 2)
                start = late + late % 2
                pairs = (TILES - start) // 2
                with eng.Fori(0, pairs) as r:
                    for u in range(2):
                        for piece, lag in order:
                            body(piece, r * 2 + (start + u - lag), (start + u - lag) % 2)
                for i in range(TILES, TILES + late):
                    for piece, lag in order:
                        if i - lag < TILES:
                            body(piece, i - lag, (i - lag) % 2)

            def tile_of(x, i):
                return x[:, bass.ds(i, 1), :].rearrange("p a c -> p (a c)") if not isinstance(i, int) else x[:, i, :]

            with nc.Block() as block:
                @block.sync
                def _(sp):
                    sp.dma_start(WZ[:, :, :], w["wz"][d]).then_inc(loaded, 16)

                @block.gpsimd
                def _(pool):
                    def body(piece, i, p):
                        if piece == "skip":
                            pool.wait_ge(xt_read, i + 2)
                            pool.wait_ge(y_summed, i + 1)
                            nc.gpsimd.tensor_tensor(XD[:, :], XK[:, p, :], SKIP[:, :], ALU.mult).then_inc(skipped, 1)
                            return
                        pool.wait_ge(y_made, i + 1)
                        nc.gpsimd.tensor_tensor(XF[:, p, :, :], XBC[:, :, bass.ds(i * P, P)],
                                                consts["zero"][:, 0:CH * P].rearrange("p (c n) -> p c n", n=P), ALU.add)
                        nc.gpsimd.tensor_tensor(HF[:, p, :, :], HT[:, :, bass.ds(i * P, P)],
                                                consts["zero"][:, 0:2 * P].rearrange("p (c n) -> p c n", n=P),
                                                ALU.add).then_inc(copied, 1)
                    pool.sem_inc(skipped, 2)
                    pipeline(pool, body, [("skip", 1), ("copy", 0)])

                @block.tensor
                def _(pe):
                    def body(piece, i, p):
                        if piece == "turn_y":
                            pe.wait_ge(yg_made, i + 3)
                            pe.wait_ge(yt_read, i + 1)
                            for c in range(4):
                                mm = pe.transpose(pyt[:, c * P:(c + 1) * P], YG[:, p, c * P:(c + 1) * P], ident[:, :])
                            mm.then_inc(yt_made, 1)
                        if piece == "front":
                            pe.wait_ge(copied, i + 1)
                            pe.wait_ge(m_made, i + 1)
                            pe.matmul(pcb[:, :], XF[:, p, 4, :], XF[:, p, 5, :], start=True, stop=True).then_inc(cb_made, 1)
                            pe.wait_ge(xt_read, i + 1)
                            for c in range(4):
                                mm = pe.transpose(pxt[:, c * P:(c + 1) * P], XF[:, p, c, :], ident[:, :])
                            mm.then_inc(xt_made, 1)
                            pe.wait_ge(sz_made, i + 1)
                            for k in range(2):
                                mm = pe.matmul(pz[:, :], HF[:, p, k, :], WZ[:, k, :], start=(k == 0), stop=(k == 1))
                            mm.then_inc(z_made, 1)
                        if piece == "y":
                            pe.wait_ge(yg_made, i + 1)
                            pe.wait_ge(m_made, i + 2)
                            pe.wait_ge(xt_read, i + 2)
                            for h in range(NH):
                                mm = pe.matmul(py[p][:, h * HD:(h + 1) * HD], M[:, p, h, :], XK[:, p, h * HD:(h + 1) * HD],
                                               start=True, stop=True)
                            mm.then_inc(y_made, 1)
                        if piece == "out":
                            pe.wait_ge(yt_read, i + 2)
                            pe.wait_ge(ou_made, i + 1)
                            for c in range(4):
                                mm = pe.matmul(po[:, :], YT[:, c * P:(c + 1) * P], WO[:, c, :], start=(c == 0), stop=(c == 3))
                            mm.then_inc(out_made, 1)

                    pe.sem_inc(y_made, 2)
                    pe.sem_inc(yt_made, 2)
                    pe.sem_inc(out_made, 1)
                    pe.wait_ge(loaded, 16)
                    pipeline(pe, body, [("turn_y", 2), ("y", 1), ("front", 0), ("out", 2)])

                @block.scalar
                def _(act):
                    a = nc.scalar

                    def body(piece, i, p):
                        if piece == "turned_y":
                            act.wait_ge(yt_made, i + 3)
                            act.wait_ge(out_made, i + 1)
                            a.activation(YT[:, :], pyt[:, :], ACT.Copy).then_inc(yt_read, 1)
                        if piece == "front":
                            act.wait_ge(xt_made, i + 1)
                            act.wait_ge(y_made, i + 1)
                            act.wait_ge(skipped, i + 1)
                            a.activation(XK[:, p, :], pxt[:, :], ACT.Copy).then_inc(xt_read, 1)
                            act.wait_ge(z_made, i + 1)
                            act.wait_ge(yg_made, i + 1)
                            a.activation(SZ[:, p, :], pz[:, :], ACT.Silu).then_inc(sz_made, 1)
                        if piece == "square":
                            act.wait_ge(yg_made, i + 3)
                            act.wait_ge(ms_made, i + 1)
                            if not isinstance(i, int) or i:
                                act.wait_ge(sq_made, i + 2)
                            a.activation(SQ[:, :], YG[:, p, :], ACT.Square, accum_out=MSJ[:, p:p + 1]).then_inc(sq_made, 1)

                    act.sem_inc(sz_made, 1)
                    act.sem_inc(xt_read, 1)
                    act.sem_inc(yt_read, 1)
                    act.sem_inc(sq_made, 2)
                    pipeline(act, body, [("turned_y", 2), ("front", 0), ("square", 1)])

                @block.vector
                def _(dve):
                    v = nc.vector

                    def body(piece, i, p):
                        if piece == "m":
                            dve.wait_ge(cb_made, i + 1)
                            dve.wait_ge(y_made, i + 1)
                            for q in range(QUADS):
                                r = slice(q * L, (q + 1) * L)
                                pm = PM[r, bass.ds(i, 1), :] if not isinstance(i, int) else PM[r, i:i + 1, :]
                                mm = v.tensor_tensor(M[r, p, :, r], pm.rearrange("p a (h l) -> p (a h) l", l=L),
                                                     pcb[r, r].unsqueeze(1).broadcast_to([L, NH, L]), ALU.mult)
                            mm.then_inc(m_made, 1)
                        if piece == "gate":
                            dve.wait_ge(y_made, i + 3)
                            dve.wait_ge(sz_made, i + 2)
                            dve.wait_ge(yt_made, i + 1)
                            dve.wait_ge(sq_made, i + 1)
                            dve.wait_ge(skipped, i + 3)
                            v.tensor_tensor(YG[:, p, :], py[p][:, :], XD[:, :], ALU.add).then_inc(y_summed, 1)
                            dve.wait_ge(y_summed, i + 2)
                            v.tensor_tensor(YG[:, p, :], YG[:, p, :], SZ[:, p, :], ALU.mult).then_inc(yg_made, 1)
                        if piece == "out":
                            dve.wait_ge(sq_made, i + 3)
                            ms = MS[:, bass.ds(i, 1)] if not isinstance(i, int) else MS[:, i:i + 1]
                            v.tensor_scalar(ms, MSJ[:, p:p + 1], 1.0 / 512, 1e-5, ALU.mult, ALU.add).then_inc(ms_made, 1)
                            dve.wait_ge(out_made, i + 2)
                            v.tensor_scalar(tile_of(OU, i), po[:, :], 1.0, None, ALU.mult).then_inc(ou_made, 1)

                    v.memset(M[:, :, :, :], 0.0).then_inc(m_zeroed, 1)
                    dve.wait_ge(m_zeroed, 1)
                    dve.sem_inc(m_made, 1)
                    dve.sem_inc(yg_made, 2)
                    dve.sem_inc(y_summed, 1)
                    dve.sem_inc(ou_made, 1)
                    dve.sem_inc(ms_made, 2)
                    pipeline(dve, body, [("gate", 1), ("m", 0), ("out", 2)])


def mamba2_layer(nc, name, H, XT, ident, w, consts):
    with Stage(nc, name) as st:
        HT = st.sb("HT", [P, 2, T])
        GATE = st.sb("GATE", [P, TILES, 256])
        MS = [st.sb(f"MS{d}", [P, TILES]) for d in range(2)]
        cc = {n: st.sb(n, shape) for n, shape in (("blocks", [P, P]), ("own", [P, GROUP]), ("zero", [P, 6 * P]))}
        with Stage(nc, name + "p") as sp_:
            XN = sp_.sb("XN", [P, TILES, P])
            normalise(nc, name + "n", H, XT, ident, XN)
            WP = sp_.sb("WP", [P, 256])
            PB = sp_.sb("PB", [P, 256])
            GB = sp_.sb("GB", [P, 2, 256])
            PRE = sp_.sb("PRE", [P, TILES, 256])
            psum = Stage(nc, name + "pp")
            psum.__enter__()
            pp = psum.ps("pp", [P, TILES, 256])
            loaded = sp_.sem("loaded")
            made = sp_.sem("made")
            zeroed = sp_.sem("zeroed")
            with nc.Block() as block:
                @block.sync
                def _(sp):
                    sp.dma_start(WP[:, :], w["pre_w"]).then_inc(loaded, 16)
                    sp.dma_start(PB[:, :], w["pre_b"].partition_broadcast(P)).then_inc(loaded, 16)
                    sp.dma_start(GB[:, 0, :], w["pre_ln_g"].partition_broadcast(P)).then_inc(loaded, 16)
                    sp.dma_start(GB[:, 1, :], w["pre_ln_b"].partition_broadcast(P)).then_inc(loaded, 16)
                    sp.dma_start(cc["blocks"][:, :], consts["c_blocks"]).then_inc(loaded, 16)
                    sp.dma_start(cc["own"][:, :], consts["c_own"]).then_inc(loaded, 16)
                    sp.wait_ge(loaded, 96)

                @block.gpsimd
                def _(pool):
                    nc.gpsimd.memset(cc["zero"][:, :], 0.0).then_inc(zeroed, 1)
                    nc.gpsimd.tensor_tensor(H[:, :, :], H[:, :, :], XN[:, :, :], ALU.add).then_inc(zeroed, 1)

                @block.tensor
                def _(pe):
                    pe.wait_ge(loaded, 96)
                    for t in range(TILES):
                        pe.matmul(pp[:, t, :], XT[:, t * P:(t + 1) * P], WP[:, :], start=True, stop=True).then_inc(made, 1)

                @block.vector
                def _(dve):
                    dve.wait_ge(loaded, 96)
                    for g in range(GROUPS):
                        s = slice(g * GT, (g + 1) * GT)
                        dve.wait_ge(made, (g + 1) * GT)
                        nc.vector.tensor_tensor(PRE[:, s, :], pp[:, s, :], PB[:, :].unsqueeze(1).broadcast_to([P, GT, 256]),
                                                ALU.add)

            psum.__exit__(None, None, None)
            layer_norm(nc, name + "pl", PRE, TILES, 256, GB, 1e-5)
            turn_256(nc, name + "pt", PRE, HT, ident, GATE)

        OU = [st.sb(f"OU{d}", [P, TILES, 256]) for d in range(2)]
        for d, back in enumerate((False, True)):
            mamba2_direction(nc, f"{name}{'fb'[d]}", HT, OU[d], MS[d], ident, cc, w, d, back)

        with Stage(nc, name + "o") as so:
            WO = so.sb("WO", [P, 2, P])
            GB = so.sb("GB", [P, 3, P])
            RT = so.sb("RT", [P, 2, TILES])
            Y = so.sb("Y", [P, TILES, P])
            loaded = so.sem("loaded")
            root_made = so.sem("root_made")
            chain = so.sem("chain")
            with nc.Block() as block:
                @block.sync
                def _(sp):
                    sp.dma_start(WO[:, :, :], w["post_w"]).then_inc(loaded, 16)
                    for n, src in enumerate(("post_ln_g", "post_ln_b", "post_b")):
                        sp.dma_start(GB[:, n, :], w[src].partition_broadcast(P)).then_inc(loaded, 16)
                    sp.wait_ge(loaded, 64)

                @block.scalar
                def _(act):
                    for d in range(2):
                        nc.scalar.activation(RT[:, d, :], MS[d][:, :], ACT.Sqrt).then_inc(root_made, 1)

                @block.vector
                def _(dve):
                    v = nc.vector
                    link = Chain(dve, chain)
                    dve.wait_ge(root_made, 2)
                    link(v.reciprocal(RT[:, :, :], RT[:, :, :]))
                    for d in range(2):
                        link(v.tensor_tensor(OU[d][:, :, :], OU[d][:, :, :], spread(RT[:, d, :], 256), ALU.mult))
                    link(v.tensor_tensor(OU[0][:, :, :], OU[0][:, :, :], OU[1][:, :, :], ALU.add))
                    link(v.tensor_tensor(OU[0][:, :, :], OU[0][:, :, :], GATE[:, :, :], ALU.mult))

            turn_256(nc, name + "ot", OU[0], HT, ident)
            with Stage(nc, name + "q") as sq:
                po = sq.ps("po", [P, TILES, P])
                made = sq.sem("made")
                with nc.Block() as block:
                    @block.tensor
                    def _(pe):
                        for t in range(TILES):
                            for k in range(2):
                                mm = pe.matmul(po[:, t, :], HT[:, k, t * P:(t + 1) * P], WO[:, k, :],
                                               start=(k == 0), stop=(k == 1))
                            mm.then_inc(made, 1)

                    @block.vector
                    def _(dve):
                        for g in range(GROUPS):
                            s = slice(g * GT, (g + 1) * GT)
                            dve.wait_ge(made, (g + 1) * GT)
                            nc.vector.tensor_tensor(Y[:, s, :], po[:, s, :], GB[:, 2, :].unsqueeze(1).broadcast_to([P, GT, P]),
                                                    ALU.add)
            layer_norm(nc, name + "ol", Y, TILES, P, GB, 1e-5, H)


CONSTS = dict(ident=([P, P], F32), iota=([P, 64], F32), sel1=([96, 32, P], BF16),
              pick=([P, 8 + 2 * TILES], F32), sel2=([96, 16, P], BF16), earlier=([P, 2, P], BF16))


def build(nc, ins, out):
    Stage.spent = []
    with Stage(nc, "g") as st:
        H = st.sb("H", [P, TILES, P])
        XT = st.sb("XT", [P, T])
        consts = {n: st.sb(n, shape, dt) for n, (shape, dt) in CONSTS.items()}
        ident, iota, sel1 = consts["ident"], consts["iota"], consts["sel1"]
        with Stage(nc, "start") as s0:
            loaded = s0.sem("loaded")
            with nc.Block() as block:
                @block.sync
                def _(sp):
                    n = 0
                    for name, tile in consts.items():
                        sp.dma_start(tile[:], ins["c_" + name]).then_inc(loaded, 16)
                        n += 16
                    sp.wait_ge(loaded, n)

        def relu_layer(name, E, K, wr, br, w12, b2):
            normalise(nc, name + "n", H, XT, ident)
            with Stage(nc, name + "s") as s:
                OT = s.sb("OT", [P, T])
                XR = s.sb("XR", [P, 2, T], F32R)
                gateT = s.sb("gateT", [96, T], BF16)
                gateF = s.sb("gateF", [E, T])
                weights = Weights(nc, s, ins[w12], 2, 8 * P, 4)
                route_softmax(nc, name + "r", XT, XR, ident, iota, ins[wr], ins[br], E, K, gateT, gateF, weights, relu_bias)
                relu_experts(nc, name + "x", XR, OT, gateT, gateF, sel1, weights, ins[b2], E)
                add_turned(nc, name + "a", H, OT, ident)

        choose_tokens(nc, "tok", H, ins["x"], ins["x"].rearrange("s t d -> (s t) d"), ins["L0_tok_W"],
                      ins["L0_tok_b"], ident, consts["pick"])
        recycle(nc)
        with Stage(nc, "t0") as s:
            AT = s.sb("AT", [P, TILES, P])
            normalise(nc, "t0n", H, XT, ident, AT)
            bimamba_layers(nc, "t0x", H, XT, AT, ident, sel1,
                           {n: ins["L0_attn_" + n] for n in ("in", "bcd", "dt", "v", "a", "out", "ln")})
        recycle(nc)
        normalise(nc, "m0n", H, XT, ident)
        with Stage(nc, "m0s") as s:
            OT = s.sb("OT", [P, T])
            XR = s.sb("XR", [P, 2, T], F32R)
            gateT = s.sb("gateT", [96, 2, T], BF16)
            weights = Weights(nc, s, ins["L0_units"], 4, 3 * P, 0)
            route_grouped(nc, "m0r", XT, XR, ident, iota, consts["earlier"], ins["L0_ffn_gate_w"], ins["L0_ffn_gate_b"],
                          gateT, weights)
            gated_experts(nc, "m0x", XR, OT, gateT, None, consts["sel2"], lambda u, i, j: u, weights,
                          None, 2, False)
            add_turned(nc, "m0a", H, OT, ident)
        recycle(nc)
        mamba2_layer(nc, "t1x", H, XT, ident, {n[8:]: ap for n, ap in ins.items() if n.startswith("L1_attn_")}, ins)
        recycle(nc)
        relu_layer("m1", 16, 4, "L1_ffn_router_w", "L1_ffn_router_b", "L1_w12", "L1_ffn_b2")
        recycle(nc)
        with Stage(nc, "t2") as s:
            XN = s.sb("XN", [P, TILES, P])
            normalise(nc, "t2n", H, XT, ident, XN)
            attend(nc, "t2x", H, XT, XN, ident, *(ins["L2_attn_" + n] for n in ("W_q", "W_k", "W_v", "W_o", "ln_gamma", "ln_beta")))
        recycle(nc)
        relu_layer("m2", 8, 1, "L2_ffn_Wr", "L2_ffn_br", "L2_w12", "L2_ffn_b2")
        recycle(nc)
        normalise(nc, "t3n", H, XT, ident)
        gated_recurrence(nc, "t3x", H, XT, ident, {n: ins["L3_attn_" + n] for n in
                                                   ("Wq", "Wk", "Wg", "Wgk1", "Wgk2", "bgk2", "Wo", "units")})
        recycle(nc)
        normalise(nc, "m3n", H, XT, ident)
        with Stage(nc, "m3s") as s:
            OT = s.sb("OT", [P, T])
            XR = s.sb("XR", [P, 2, T], F32R)
            gateT = s.sb("gateT", [96, 1, T], BF16)
            gateF = s.sb("gateF", [8, T])
            weights = Weights(nc, s, ins["L3_units"], 4, 2 * P, 3)
            route_softmax(nc, "m3r", XT, XR, ident, iota, ins["L3_ffn_router_w"], ins["L3_ffn_router_b"], 8, 2,
                          gateT[:, 0, :], gateF, weights, quick_bias)
            gated_experts(nc, "m3x", XR, OT, gateT, gateF, sel1, lambda u, i, j: i * 2 + j // 2, weights,
                          ins["L3_ffn_down_proj_bias"], 1, True)
            add_turned(nc, "m3a", H, OT, ident)
        recycle(nc)
        with Stage(nc, "end") as s0:
            stored = s0.sem("stored")
            with nc.Block() as block:
                @block.sync
                def _(sp):
                    sp.dma_start(out, H[:, :, :]).then_inc(stored, 16)
                    sp.wait_ge(stored, 16)


def lay_out(inputs):
    a = {k: np.ascontiguousarray(v) for k, v in inputs.items()}
    d = {"x": a["x"]}
    for n in ("L1_ffn_router_w", "L1_ffn_router_b", "L1_ffn_b2", "L2_ffn_Wr", "L2_ffn_br", "L2_ffn_b2"):
        d[n] = a[n]
    for n, src in (("L1", ("L1_ffn_w1", "L1_ffn_b1", "L1_ffn_w2")), ("L2", ("L2_ffn_W1", "L2_ffn_b1", "L2_ffn_W2"))):
        w1, b1, w2 = (a[s] for s in src)
        E = w1.shape[0]
        d[n + "_w12"] = np.concatenate([w1, w2.reshape(E, 4, P, P).transpose(0, 2, 1, 3).reshape(E, P, 4 * P),
                                        b1.reshape(E, 4, P).transpose(0, 2, 1)], axis=2)
    d["L0_tok_W"], d["L0_tok_b"] = a["L0_tok_W"], a["L0_tok_b"]
    for n in ("W_k", "W_v", "W_o"):
        d["L2_attn_" + n] = a["L2_attn_" + n].T
    for n in ("ln_gamma", "ln_beta"):
        d["L2_attn_" + n] = a["L2_attn_" + n]
    wq = np.zeros((P, 8, P), np.float32)
    for h in range(8):
        wq[:, h, 16 * h:16 * h + 16] = a["L2_attn_W_q"].T[:, 16 * h:16 * h + 16]
    d["L2_attn_W_q"] = wq
    blocks = np.arange(P)[:, None]
    d["c_pick"] = np.concatenate([blocks % 8 == np.arange(8), blocks // 8 == np.arange(TILES), blocks * P,
                                  np.zeros((P, TILES - 1))], axis=1).astype(np.float32)
    m = {n: a["L0_attn_" + n] for n in ("in_proj_w", "conv_w", "conv_b", "xproj_w", "dtproj_w", "dtproj_b", "A_log",
                                        "Dskip", "out_proj_w", "ln_w", "ln_b")}
    d["L0_attn_in"] = m["in_proj_w"].reshape(4, 4, P, P).transpose(0, 3, 1, 2)
    xp = m["xproj_w"].reshape(4, 2, 40, 2, P).transpose(0, 1, 4, 3, 2)
    d["L0_attn_bcd"] = np.concatenate([xp[..., 8:40]] * 3 + [xp[..., 0:8]], axis=-1)
    d["L0_attn_dt"] = m["dtproj_w"].reshape(4, 2, 2, P, 8).transpose(0, 1, 4, 2, 3)

    def per_channel(w):
        return w.reshape(4, 2, 2, P, -1).transpose(0, 1, 3, 2, 4)

    d["L0_attn_v"] = np.concatenate([per_channel(m[n]) for n in ("conv_w", "conv_b", "dtproj_b", "Dskip")], axis=-1)
    d["L0_attn_a"] = per_channel(m["A_log"])
    d["L0_attn_out"] = m["out_proj_w"].reshape(4, P, 2, P).transpose(0, 3, 2, 1)
    d["L0_attn_ln"] = np.stack([m["ln_w"][:, 0], m["ln_b"][:, 0]], axis=1)
    m = {n[8:]: v for n, v in a.items() if n.startswith("L1_attn_")}
    for n in ("pre_w", "pre_b", "pre_ln_g", "pre_ln_b", "post_b", "post_ln_g", "post_ln_b"):
        d["L1_attn_" + n] = m[n]
    d["L1_attn_post_w"] = m["post_w"].reshape(2, P, P).transpose(1, 0, 2)
    both = {n: np.stack([m[n + "_f"], m[n + "_b"]]) for n in ("win", "convw", "convb", "dtb", "Alog", "D", "normw", "wout")}
    win = both["win"].reshape(2, 2, P, 1288).transpose(0, 2, 1, 3)
    d["L1_attn_wz"], d["L1_attn_wx"], d["L1_attn_wt"] = win[..., :512], win[..., 512:1280], win[..., 1280:]
    d["L1_attn_db"] = np.stack([both["dtb"], both["Alog"]], axis=1)
    d["L1_attn_skip"] = np.repeat(both["D"], 64, axis=1)
    d["L1_attn_v"] = np.concatenate([both["convw"], both["convb"][..., None]],
                                    axis=-1).reshape(2, 6, P, 5).transpose(0, 2, 1, 3)
    d["L1_attn_wo"] = both["wout"].reshape(2, 4, P, 256).transpose(0, 2, 1, 3)
    d["L1_attn_nw"] = both["normw"].reshape(2, 4, P).transpose(0, 2, 1)
    p = np.arange(P)
    d["c_blocks"] = (p[:, None] // L == p[None, :] // L).astype(np.float32)
    d["c_own"] = (p[:, None] % L == np.arange(GROUP)[None, :] % L).astype(np.float32)
    d["L0_ffn_gate_w"], d["L0_ffn_gate_b"] = a["L0_ffn_gate_w"].T, a["L0_ffn_gate_b"]

    def two(w):
        return w.reshape(32, 2, P, 64).transpose(0, 2, 1, 3).reshape(32, P, P)

    d["L0_units"] = np.concatenate([two(a["L0_ffn_w1"]), two(a["L0_ffn_w3"]), a["L0_ffn_w2"].reshape(32, P, P)], axis=2)
    for n in ("Wq", "Wk", "Wgk2"):
        d["L3_attn_" + n] = np.concatenate([a["L3_attn_" + n]] * 2, axis=1)
    d["L3_attn_bgk2"] = np.concatenate([a["L3_attn_bgk2"]] * 2)[:, None]
    for n in ("Wg", "Wgk1", "Wo"):
        d["L3_attn_" + n] = a["L3_attn_" + n]
    lane = np.arange(P)
    column = (lane // 16 % 4) * 32 + lane // 64 * 16 + np.arange(16)[:, None]
    values = a["L3_attn_Wv"][:, column].transpose(1, 0, 2)
    gather = (column[:, :, None] == np.arange(P)[None, None, :]).astype(np.float32)
    d["L3_attn_units"] = np.concatenate([values, gather], axis=2)
    for n in ("router_w", "router_b", "down_proj_bias"):
        d["L3_ffn_" + n] = a["L3_ffn_" + n]
    gu = a["L3_ffn_gate_up_proj"].reshape(8, P, 2, 2, P).transpose(0, 3, 1, 2, 4).reshape(16, P, 2 * P)
    gub = a["L3_ffn_gate_up_proj_bias"].reshape(8, 2, 2, P).transpose(0, 2, 3, 1).reshape(16, P, 2)
    d["L3_units"] = np.concatenate([gu, a["L3_ffn_down_proj"].reshape(16, P, P), gub], axis=2)
    c = np.arange(P)[None, None, :] // 64
    d["c_sel2"] = (np.arange(96)[:, None, None] % 32 == 2 * np.arange(16)[None, :, None] + c).astype(mybir.dt.np(BF16))
    tri = np.arange(P)[:, None] < np.arange(P)[None, :]
    d["c_earlier"] = np.stack([tri, np.ones_like(tri)], axis=1).astype(mybir.dt.np(BF16))
    d["c_ident"] = np.eye(P, dtype=np.float32)
    d["c_iota"] = np.broadcast_to(np.arange(64, dtype=np.float32), (P, 64))
    r = np.arange(96)[:, None, None] % 32
    d["c_sel1"] = np.broadcast_to(r == np.arange(32)[None, :, None], (96, 32, P)).astype(mybir.dt.np(BF16))
    return {k: np.ascontiguousarray(v) for k, v in d.items()}


def kernel(**inputs):
    import concourse.bacc as bacc
    from concourse.bass_utils import run_bass_kernel_spmd

    nc = bacc.Bacc("TRN2", target_bir_lowering=False, num_devices=1)
    arrays = lay_out(inputs)
    ins = {n: nc.dram_tensor("in_" + n, a.shape, mybir.dt.from_np(a.dtype), kind="ExternalInput").ap()
           for n, a in arrays.items()}
    out = nc.dram_tensor("out", (P, TILES, P), F32, kind="ExternalOutput").ap()
    build(nc, ins, out)
    r = run_bass_kernel_spmd(nc, [{"in_" + n: a for n, a in arrays.items()}], core_ids=[0])
    return r.results[0]["out"].transpose(1, 0, 2).reshape(SEQS, L, P)
```
